# Optimizing a Trainium2 kernel written in Bass

```python
import numpy as np
import jax
import jax.numpy as jnp

def _softmax(x, axis=-1):
    return jax.nn.softmax(x, axis=axis)

def _gelu(x):
    return jax.nn.gelu(x, approximate=True)

def _silu(x):
    return jax.nn.silu(x)

def _sigmoid(x):
    return jax.nn.sigmoid(x)

def _layernorm(x, axis=-1, eps=1e-05):
    m = jnp.mean(x, axis=axis, keepdims=True)
    v = jnp.var(x, axis=axis, keepdims=True)
    return (x - m) / jnp.sqrt(v + eps)

def _scatter_add(tgt, idx, src, axis=0):
    return tgt.at[idx].add(src)

def _segment_sum(src, seg, n):
    return jax.ops.segment_sum(src, seg, n)
kernel_name = 'mk_gnn_resnorm_d2_gnn_r8_122367'

def setup_inputs(seed: int=0):
    np.random.seed(seed)
    _w = jnp.asarray

    def _rec_inputs():
        import jax
        import jax.numpy as jnp
        _gk = jax.random.key(seed)
        x = -0.0003713 + 1 * jax.random.normal(jax.random.fold_in(_gk, 1), (12500, 128), jnp.float32)
        _s = jax.random.randint(jax.random.fold_in(_gk, 2), (200000,), 0, 12500, jnp.int32)
        _d = jax.random.randint(jax.random.fold_in(_gk, 3), (200000,), 0, 12500, jnp.int32)
        _loop = jnp.arange(12500, dtype=jnp.int32)
        src = jnp.concatenate([_s, _d, _loop])
        dst = jnp.concatenate([_d, _s, _loop])
        _o = jnp.argsort(dst, stable=True)
        src = src[_o]
        dst = dst[_o]
        edge_attr_32 = jax.random.uniform(jax.random.fold_in(_gk, 11), (412500, 32), jnp.float32, 0.0, 1)
        edge_weight = jax.random.uniform(jax.random.fold_in(_gk, 13), (412500,), jnp.float32, 0.0, 0.999999)
        return (x, src, dst, edge_attr_32, edge_weight)
    x, src, dst, edge_attr_32, edge_weight = _rec_inputs()

    def _L0_gnn_setup():
        import jax, jax.numpy as jnp
        import numpy as np
        LOG2 = float(np.log(2.0))

        def ssp(v):
            return jax.nn.softplus(v) - jnp.asarray(LOG2, v.dtype)
        key = jax.random.key(seed)
        ks = jax.random.split(key, 16)
        N, B, F, R, P = (12500, 128, 64, 32, 200000)
        inp = {'x': jax.random.normal(ks[0], (N, B), jnp.float32), 'f_ij': jax.random.uniform(ks[1], (P, R), jnp.float32), 'rcut_ij': jax.random.uniform(ks[2], (P,), jnp.float32), 'pairlist': jax.random.randint(ks[3], (2, P), 0, N, jnp.int64), 'w_in': jax.random.normal(ks[4], (B, F), jnp.float32) * (1.0 / np.sqrt(B)), 'b_in': jnp.zeros((F,), jnp.float32), 'w_f1': jax.random.normal(ks[5], (R, F), jnp.float32) * (1.0 / np.sqrt(R)), 'b_f1': jnp.zeros((F,), jnp.float32), 'w_f2': jax.random.normal(ks[6], (F, F), jnp.float32) * (1.0 / np.sqrt(F)), 'b_f2': jnp.zeros((F,), jnp.float32), 'w_o1': jax.random.normal(ks[7], (F, B), jnp.float32) * (1.0 / np.sqrt(F)), 'b_o1': jnp.zeros((B,), jnp.float32), 'w_o2': jax.random.normal(ks[8], (B, B), jnp.float32) * (1.0 / np.sqrt(B)), 'b_o2': jnp.zeros((B,), jnp.float32)}
        return inp
    _L0_gnn_all = _L0_gnn_setup()
    _L0_gnn_in = {k: v for k, v in _L0_gnn_all.items() if k in ('w_in', 'b_in', 'w_f1', 'b_f1', 'w_f2', 'b_f2', 'w_o1', 'b_o1', 'w_o2', 'b_o2')}
    del _L0_gnn_all

    def _L1_gnn_setup():
        import jax, jax.numpy as jnp
        import numpy as np
        N_NODES = 12500
        N_EDGES = 400000
        D_IN = 128
        D_OUT = 128
        BN_EPS = 1e-05
        key = jax.random.key(seed)
        k1, k2, k3, k4 = jax.random.split(key, 4)
        x = jax.random.normal(k1, (N_NODES, D_IN), dtype=jnp.float32)
        edge_index = jax.random.randint(k2, (2, N_EDGES), 0, N_NODES, dtype=jnp.int64)
        W = jax.random.normal(k3, (D_IN, D_OUT), dtype=jnp.float32) / np.sqrt(D_IN)
        b = jnp.zeros((D_OUT,), dtype=jnp.float32)
        gamma = jnp.ones((D_OUT,), dtype=jnp.float32)
        beta = jnp.zeros((D_OUT,), dtype=jnp.float32)
        return {'x': x, 'edge_index': edge_index, 'W': W, 'b': b, 'gamma': gamma, 'beta': beta}
    _L1_gnn_all = _L1_gnn_setup()
    _L1_gnn_in = {k: v for k, v in _L1_gnn_all.items() if k in ('W', 'b', 'gamma', 'beta')}
    del _L1_gnn_all
    return {'x': x, 'src': src, 'dst': dst, 'edge_attr_32': edge_attr_32, 'edge_weight': edge_weight, 'L0_gnn_w_in': _L0_gnn_in['w_in'], 'L0_gnn_b_in': _L0_gnn_in['b_in'], 'L0_gnn_w_f1': _L0_gnn_in['w_f1'], 'L0_gnn_b_f1': _L0_gnn_in['b_f1'], 'L0_gnn_w_f2': _L0_gnn_in['w_f2'], 'L0_gnn_b_f2': _L0_gnn_in['b_f2'], 'L0_gnn_w_o1': _L0_gnn_in['w_o1'], 'L0_gnn_b_o1': _L0_gnn_in['b_o1'], 'L0_gnn_w_o2': _L0_gnn_in['w_o2'], 'L0_gnn_b_o2': _L0_gnn_in['b_o2'], 'L1_gnn_W': _L1_gnn_in['W'], 'L1_gnn_b': _L1_gnn_in['b'], 'L1_gnn_gamma': _L1_gnn_in['gamma'], 'L1_gnn_beta': _L1_gnn_in['beta']}

def reference(x, src, dst, edge_attr_32, edge_weight, L0_gnn_w_in, L0_gnn_b_in, L0_gnn_w_f1, L0_gnn_b_f1, L0_gnn_w_f2, L0_gnn_b_f2, L0_gnn_w_o1, L0_gnn_b_o1, L0_gnn_w_o2, L0_gnn_b_o2, L1_gnn_W, L1_gnn_b, L1_gnn_gamma, L1_gnn_beta):
    import jax
    import jax.numpy as jnp

    def _L0_gnn_ref(x, f_ij, rcut_ij, pairlist, w_in, b_in, w_f1, b_f1, w_f2, b_f2, w_o1, b_o1, w_o2, b_o2):
        import jax, jax.numpy as jnp
        import numpy as np
        LOG2 = float(np.log(2.0))

        def ssp(v):
            return jax.nn.softplus(v) - jnp.asarray(LOG2, v.dtype)
        n_atoms = x.shape[0]
        h = x @ w_in + b_in
        Wij = ssp(f_ij @ w_f1 + b_f1) @ w_f2 + b_f2
        Wij = Wij * rcut_ij[:, None]
        idx_i, idx_j = (pairlist[0], pairlist[1])
        x_ij = h[idx_j] * Wij
        agg = jax.ops.segment_sum(x_ij, idx_i, num_segments=n_atoms)
        out = ssp(agg @ w_o1 + b_o1) @ w_o2 + b_o2
        return out

    def _L1_gnn_ref(x, edge_index, W, b, gamma, beta):
        import jax, jax.numpy as jnp
        import numpy as np
        N_NODES = 12500
        N_EDGES = 400000
        D_IN = 128
        D_OUT = 128
        BN_EPS = 1e-05
        N = x.shape[0]
        xw = x @ W
        loop = jnp.arange(N, dtype=edge_index.dtype)
        src = jnp.concatenate([edge_index[0], loop])
        dst = jnp.concatenate([edge_index[1], loop])
        deg = jax.ops.segment_sum(jnp.ones_like(dst, dtype=xw.dtype), dst, num_segments=N)
        dinv = jnp.where(deg > 0, jax.lax.rsqrt(deg), 0.0)
        norm = dinv[src] * dinv[dst]
        msg = xw[src] * norm[:, None]
        out = jax.ops.segment_sum(msg, dst, num_segments=N) + b
        mean = jnp.mean(out, axis=0)
        var = jnp.mean((out - mean) ** 2, axis=0)
        out = (out - mean) * jax.lax.rsqrt(var + BN_EPS) * gamma + beta
        return jax.nn.relu(out)
    edge_index = jnp.stack([src, dst])
    x = _layernorm(x + _L0_gnn_ref(x, edge_attr_32, edge_weight, edge_index, L0_gnn_w_in, L0_gnn_b_in, L0_gnn_w_f1, L0_gnn_b_f1, L0_gnn_w_f2, L0_gnn_b_f2, L0_gnn_w_o1, L0_gnn_b_o1, L0_gnn_w_o2, L0_gnn_b_o2), axis=-1)
    x = _layernorm(x + _L1_gnn_ref(x, edge_index, L1_gnn_W, L1_gnn_b, L1_gnn_gamma, L1_gnn_beta), axis=-1)
    return x

_drawn_inputs = setup_inputs


def setup_inputs(seed=0):
    import zlib

    import numpy as np

    out = dict(_drawn_inputs(seed))
    spreads = {'L0_gnn_b_in': (0.0, 0.1),
     'L0_gnn_b_f1': (0.0, 0.1),
     'L0_gnn_b_f2': (0.0, 0.1),
     'L0_gnn_b_o1': (0.0, 0.1),
     'L0_gnn_b_o2': (0.0, 0.1),
     'L1_gnn_b': (0.0, 0.1),
     'L1_gnn_gamma': (1.0, 0.2),
     'L1_gnn_beta': (0.0, 0.1)}
    factors = {}
    for name, (base, spread) in spreads.items():
        noise = np.random.default_rng([zlib.crc32(name.encode()), seed]).standard_normal(out[name].shape)
        drawn = base * np.exp(spread * noise) if base else spread * noise
        out[name] = jnp.asarray(drawn.astype(out[name].dtype))
    for name, factor in factors.items():
        out[name] = (out[name] * factor).astype(out[name].dtype)
    return out
```

```python
from contextlib import ExitStack

import concourse.bass as bass
from concourse import mybir

F32 = mybir.dt.float32
BF16 = mybir.dt.bfloat16
I32 = mybir.dt.int32
U32 = mybir.dt.uint32
ALU = mybir.AluOpType
ACT = mybir.ActivationFunctionType
AX = mybir.AxisListType

P = 128
N, E = 12500, 412500
D, F, R = 128, 64, 32
J = 8
GE = J * P
G = -(-E // GE)
SEEN = G * GE - E
GC = -(-G // P)
GPAD = 416
PAD_NODE = N
TRASH = N + 1
NT = 99 * P
K = 4
NP, NC = 125, 100
B = 4
NB = NC // B
BW = B * NP
LN_EPS = BN_EPS = 1e-5
ZERO_COLS = 1056
ZEROED = 48
WORK = 11800


def ready(g, depth):
    return g + 1 + depth


def free(g):
    return g + 1


def over(eng, n, body):
    with eng.Fori(0, n // 2) as i:
        body(2 * i, 0, i)
        body(2 * i + 1, 1, i)
    if n % 2:
        body(n - 1, 0, n // 2)


def pipelined(eng, n, first, step, last):
    first(0, 0, 0)
    with eng.Fori(0, n // 2) as i:
        step(2 * i, 0, i)
        step(2 * i + 1, 1, i)
    last(n - 1, 0, n // 2)


INPUTS = {"x": "x", "src": "src", "dst": "dst", "edge_attr": "edge_attr_32", "edge_weight": "edge_weight",
          "w_in": "L0_gnn_w_in", "b_in": "L0_gnn_b_in", "w_f1": "L0_gnn_w_f1", "b_f1": "L0_gnn_b_f1",
          "w_f2": "L0_gnn_w_f2", "b_f2": "L0_gnn_b_f2", "w_o1": "L0_gnn_w_o1", "b_o1": "L0_gnn_b_o1",
          "w_o2": "L0_gnn_w_o2", "b_o2": "L0_gnn_b_o2", "W": "L1_gnn_W", "b": "L1_gnn_b",
          "gamma": "L1_gnn_gamma", "beta": "L1_gnn_beta"}


class Memory:

    def __init__(self, nc, ctx):
        def sb(name, shape, dt=F32):
            return ctx.enter_context(nc.sbuf_tensor(name, shape, dt))

        self.h_tab = nc.dram_tensor("h_tab", [NT, F], F32)
        self.y_tab = nc.dram_tensor("y_tab", [NT, D], F32)
        self.agg_tab = [nc.dram_tensor(f"agg_tab{k}", [NT, F], F32) for k in range(K)]
        self.out_tab = [nc.dram_tensor(f"out_tab{k}", [NT, D], F32) for k in range(K)]
        self.src_hl = nc.dram_tensor("src_hl", [GC * P, 2, GE], BF16)
        self.dst_hl = nc.dram_tensor("dst_hl", [GC * P, 2, GE], BF16)
        self.deg_tab = nc.dram_tensor("deg_tab", [NT], F32)
        self.dinv_tab = nc.dram_tensor("dinv_tab", [N], F32)

        self.xs = sb("xs", [NP, NC, D])
        self.arena = sb("arena", [P, NT])
        self.srcF = sb("srcF", [P, GPAD * J])
        self.dstF = sb("dstF", [P, GPAD * J])
        self.srcT = sb("srcT", [P, GPAD * J])
        self.ident = sb("ident", [P, P])
        self.below = sb("below", [P, P])
        self.iota_w = sb("iota_w", [P, P])
        self.trash = sb("trash", [P, 1])
        self.split = sb("split", [2, P], BF16)
        self.ones = sb("ones", [1, P])
        self.half = sb("half", [P, 1])
        self.base_bc = sb("base_bc", [P, GC * P])
        self.base_i = sb("base_i", [1, GC * P], I32)
        self.winid = sb("winid", [P, GC * P])
        self.flag_i = sb("flag_i", [1, 1], I32)
        self.zeros = sb("zeros", [P, ZERO_COLS])
        self.w_in_s = sb("w_in_s", [D, F])
        self.w1_s = sb("w1_s", [P, 2, P])
        self.w2_s = sb("w2_s", [P, P])
        self.wo1_s = sb("wo1_s", [F, D])
        self.wo2_s = sb("wo2_s", [D, D])
        self.W_s = sb("W_s", [D, D])
        self.bin_s = sb("bin_s", [P, F])
        self.b1_s = sb("b1_s", [P, 1])
        self.b2_s = sb("b2_s", [1, J * F])
        self.bo1_s = sb("bo1_s", [D, 1])
        self.bo2_s = sb("bo2_s", [1, B * D])
        self.gbb = sb("gbb", [D, 3])
        self.dinv = sb("dinv", [NP, NC])
        self.work = sb("work", [P, WORK])
        self.ps = ctx.enter_context(nc.psum_tensor("ps", [P, 8, 512], F32))
        self.xs_flat = self.xs.rearrange("p c d -> p (c d)")
        self.agg_added = [ctx.enter_context(nc.semaphore(f"agg_added{k}")) for k in range(K)]
        self.out_added = [ctx.enter_context(nc.semaphore(f"out_added{k}")) for k in range(K)]


def zero_table(eng, table, width, zeros, done):
    flat = table.rearrange("(p r) d -> p (r d)", p=P)
    per = NT * width // P // 3
    for t in range(3):
        n = per // ZERO_COLS
        eng.dma_start(flat[:, t * per:(t + 1) * per].rearrange("p (n c) -> p n c", n=n),
                      zeros[:, :].unsqueeze(1).to_broadcast([P, n, ZERO_COLS])).then_inc(done, 16)


def setup(nc, m, io):
    ps, work = m.ps, m.work
    ig = {"src": m.arena[:, 0:4096].bitcast(I32), "dst": m.arena[:, 4096:8192].bitcast(I32)}
    fg = {"src": m.arena[:, 8192:12288], "dst": work[:, 6000:10096]}
    given = {"src": io["src"], "dst": io["dst"]}
    cols = {"src": m.srcF, "dst": m.dstF}
    rows = {"src": m.src_hl, "dst": m.dst_hl}
    hi_i = work[:, 0:1024].bitcast(I32)
    lo_i = work[:, 1024:2048].bitcast(I32)
    hl = [work[:, 2048 + 1024 * s:3072 + 1024 * s].bitcast(BF16).rearrange("p (t e) -> p t e", t=2)
          for s in range(2)]
    xT = [work[:, 4096 + 512 * s:4096 + 512 * s + BW] for s in range(2)]
    hb = [work[0:NP, 5120 + 256 * s:5376 + 256 * s] for s in range(2)]
    xb = [work[0:NP, 10100 + 512 * s:10612 + 512 * s] for s in range(2)]
    lim = work[:, 5632:5632 + 4 * GC]
    spans = work[0:1, 5700:5700 + P]
    flag_f = work[0:1, 5900:5901]
    psT = [ps[:, 0, 0:BW], ps[:, 1, 0:BW]]
    psH = [ps[0:NP, 2, 0:B * F], ps[0:NP, 3, 0:B * F]]
    psC = [ps[:, 4, :], ps[:, 5, :]]
    psM = ps[:, 6, :]
    psS = ps[:, 7, :]
    with ExitStack() as ctx:
        def sem(name):
            return ctx.enter_context(nc.semaphore(name))
        s_x, s_w, s_wdiag, s_idx = sem("x_in"), sem("weights_in"), sem("w1_in"), {"src": sem("src_in"), "dst": sem("dst_in")}
        s_pad, s_const, s_pool = sem("pad_set"), sem("consts_set"), sem("pool_consts")
        s_fg, s_cols, s_colsdone = sem("idx_float"), sem("cols_turned"), sem("cols_copied")
        s_hl, s_hlst = sem("hl_made"), [sem("hl_stored0"), sem("hl_stored1")]
        s_int = sem("hl_ints")
        s_lim, s_limT, s_bc = sem("limits"), sem("limits_turned"), sem("bases_out")
        s_sp, s_fl, s_trash = sem("span_row"), sem("flag_steps"), sem("trash_set")
        s_xT, s_xTc, s_h, s_hb = sem("x_turned"), sem("xT_copied"), sem("h_made"), sem("h_biased")
        s_hst, s_hpad = [sem("h_stored0"), sem("h_stored1")], sem("h_pad_stored")
        s_srcT, s_turn = sem("srcT_made"), sem("turn_order")
        block = ctx.enter_context(nc.Block())
        s_xb = [sem("x_batch0"), sem("x_batch1")]
        x_rows = io["x"].rearrange("(p c) d -> p (c d)", p=NP)
        h_rows = m.h_tab[0:N, :].rearrange("(p c) d -> p (c d)", p=NP)
        NW = 14

        @block.sync
        def _(sp):
            for name in ("src", "dst"):
                a, t = given[name], ig[name]
                sp.wait_ge(s_pad, 1 if name == "src" else 2)
                full = G // P
                sp.dma_start(t.rearrange("p (c e) -> p c e", c=GC)[:, 0:full, :],
                             a[0:full * P * GE].rearrange("(c p e) -> p c e", p=P, e=GE)).then_inc(s_idx[name], 16)
                rest = G - 1 - full * P
                sp.dma_start(t[0:rest, full * GE:(full + 1) * GE],
                             a[full * P * GE:(G - 1) * GE].rearrange("(p e) -> p e", e=GE)).then_inc(s_idx[name], 16)
                sp.dma_start(t[rest:rest + 1, full * GE + SEEN:(full + 1) * GE],
                             a[(G - 1) * GE:E].rearrange("(p e) -> p e", p=1)).then_inc(s_idx[name], 16)
            sp.dma_start(m.xs_flat[:, :], io["x"].rearrange("(p c) d -> p (c d)", p=NP)).then_inc(s_x, 16)
            for n in range(2 * GC):
                name, c = ("src", "dst")[n // GC], n % GC
                sp.wait_ge(s_hl, n + 1)
                sp.dma_start(rows[name][c * P:(c + 1) * P, :, :], hl[n % 2]).then_inc(s_hlst[n % 2], 16)
            def store(q, s, turn):
                sp.wait_ge(s_hb, ready(q, 2))
                sp.dma_start(h_rows[:, bass.ds(q * (B * F), B * F)], hb[s]).then_inc(s_hst[s], 16)
            def load_x(q, s):
                sp.dma_start(xb[s], x_rows[:, bass.ds(q * (B * D), B * D)]).then_inc(s_xb[s], 16)

            def store_and_load(q, s, turn):
                store(q, s, turn)
                load_x(q + 2, s)
            load_x(0, 0)
            load_x(1, 1)
            over(sp, NB - 2, store_and_load)
            store(NB - 2, 1, NB // 2 - 1)
            store(NB - 1, 0, NB // 2)
            sp.wait_ge(s_hst[0], 16 * (NB // 2 + 1) + 32)
            sp.wait_ge(s_hst[1], 16 * (NB // 2) + 32)
            sp.wait_ge(s_x, 16)
            sp.wait_ge(s_hlst[0], 16 * GC)
            sp.wait_ge(s_hlst[1], 16 * GC)

        @block.scalar
        def _(act):
            act.wait_ge(s_const, 1)
            for t in range(4):
                act.dma_start(m.w1_s[R * t:R * t + R, t // 2, F * (t % 2):F * (t % 2) + F], io["w_f1"]).then_inc(s_wdiag, 16)
            act.dma_start(m.w_in_s[:, :], io["w_in"]).then_inc(s_w, 16)
            for t in range(2):
                act.dma_start(m.w2_s[F * t:F * t + F, F * t:F * t + F], io["w_f2"]).then_inc(s_w, 16)
                act.dma_start(m.b1_s[F * t:F * t + F, :], io["b_f1"].rearrange("(p o) -> p o", o=1)).then_inc(s_w, 16)
            act.dma_start(m.wo1_s[:, :], io["w_o1"]).then_inc(s_w, 16)
            act.dma_start(m.wo2_s[:, :], io["w_o2"]).then_inc(s_w, 16)
            act.dma_start(m.W_s[:, :], io["W"]).then_inc(s_w, 16)
            act.dma_start(m.bin_s[:, :], io["b_in"].rearrange("(o d) -> o d", o=1).to_broadcast([P, F])).then_inc(s_w, 16)
            act.dma_start(m.b2_s[:, :].rearrange("o (j d) -> o j d", j=J),
                          io["b_f2"].rearrange("(o i d) -> o i d", o=1, i=1).to_broadcast([1, J, F])).then_inc(s_w, 16)
            act.dma_start(m.bo1_s[:, :], io["b_o1"].rearrange("(p o) -> p o", o=1)).then_inc(s_w, 16)
            act.dma_start(m.bo2_s[:, :].rearrange("o (j d) -> o j d", j=B),
                          io["b_o2"].rearrange("(o i d) -> o i d", o=1, i=1).to_broadcast([1, B, D])).then_inc(s_w, 16)
            for t, v in enumerate((io["b"], io["gamma"], io["beta"])):
                act.dma_start(m.gbb[:, t:t + 1], v.rearrange("(p o) -> p o", o=1)).then_inc(s_w, 16)
            act.dma_start(m.h_tab[N:NT, :].rearrange("(p r) d -> p (r d)", r=2), m.zeros[0:(NT - N) // 2, 0:2 * F]).then_inc(s_hpad, 16)
            act.dma_start(m.y_tab[N:NT, :].rearrange("(p r) d -> p (r d)", r=2), m.zeros[0:(NT - N) // 2, 0:2 * D]).then_inc(s_hpad, 16)
            act.sem_inc(s_xTc, 2)
            def copy(q, s, turn):
                act.wait_ge(s_xT, ready(q, 0))
                act.wait_ge(s_h, free(q))
                nc.scalar.copy(xT[s], psT[s]).then_inc(s_xTc, 1)
            over(act, NB, copy)
            act.wait_ge(s_hpad, 32)
            act.wait_ge(s_w, 16 * (NW + 1))
            act.wait_ge(s_wdiag, 64)

        @block.gpsimd
        def _(pool):
            nc.gpsimd.memset(m.ident[:, :], 0.0).then_inc(s_pool, 1)
            nc.gpsimd.memset(m.below[:, :], 1.0).then_inc(s_pool, 1)
            pool.wait_ge(s_pool, 2)
            nc.gpsimd.affine_select(out=m.ident[:, :], in_=m.ident[:, :], compare_op=ALU.not_equal, fill=1.0,
                                    base=0, pattern=[[-1, P]], channel_multiplier=1).then_inc(s_pool, 1)
            nc.gpsimd.affine_select(out=m.below[:, :], in_=m.below[:, :], compare_op=ALU.is_ge, fill=0.0,
                                    base=0, pattern=[[-1, P]], channel_multiplier=1).then_inc(s_pool, 1)
            nc.gpsimd.iota(m.iota_w[:, :], [[1, P]], base=0, channel_multiplier=0,
                           allow_small_or_imprecise_dtypes=True).then_inc(s_pool, 1)
            nc.gpsimd.iota(m.trash[:, :], [[0, 1]], base=TRASH, channel_multiplier=1,
                           allow_small_or_imprecise_dtypes=True).then_inc(s_pool, 1)
            pool.wait_ge(s_const, 1)
            for k in range(K):
                zero_table(pool, m.agg_tab[k], F, m.zeros, m.agg_added[k])
            for k in range(K):
                pool.wait_ge(m.agg_added[k], ZEROED)

        @block.tensor
        def _(pe):
            pe.wait_ge(s_pool, 4)
            pe.wait_ge(s_const, 4)
            n = 0
            for a, name in enumerate(("src", "dst")):
                pe.wait_ge(s_fg, a + 1)
                v = fg[name].rearrange("p (c e j) -> p c j e", c=GC, j=J)
                for c in range(GC):
                    ng = P if (c + 1) * P <= GPAD else GPAD - c * P
                    for jh in range(2):
                        if n >= 2:
                            pe.wait_ge(s_colsdone, n - 1)
                        for j in range(4):
                            t = pe.transpose(psC[n % 2][:, P * j:P * j + ng], v[0:ng, c, 4 * jh + j, :],
                                             m.ident[0:ng, 0:ng])
                        t.then_inc(s_cols, 1)
                        n += 1
            pe.wait_ge(s_lim, 4)
            for c in range(GC):
                t = pe.matmul(psM[:, c * P:(c + 1) * P], lim[:, c:c + 1].to_broadcast([P, P]), m.ident[:, :],
                              start=True, stop=True)
            t.then_inc(s_limT, 1)
            pe.transpose(psS[0:1, 0:P], lim[:, 3 * GC:3 * GC + 1], m.ident[:, :]).then_inc(s_limT, 1)
            pe.wait_ge(s_w, 16 * (NW + 1))
            pe.sem_inc(s_h, 2)
            def turn(q, s, turn_):
                pe.wait_ge(s_xb[s], 16 * turn_ + 16)
                pe.wait_ge(s_xTc, free(q))
                for t in range(B):
                    tr = pe.transpose(psT[s][:, NP * t:NP * t + NP], xb[s][:, D * t:D * t + D],
                                      m.ident[0:NP, 0:NP])
                tr.then_inc(s_xT, 1)
                pe.wait_ge(s_xTc, ready(q, 2))
                pe.wait_ge(s_hb, free(q))
                for t in range(B):
                    mm = pe.matmul(psH[s][:, F * t:F * t + F], xT[s][:, NP * t:NP * t + NP], m.w_in_s[:, :],
                                   start=True, stop=True)
                mm.then_inc(s_h, 1)
            over(pe, NB, turn)

        @block.vector
        def _(dve):
            nc.vector.memset(m.w1_s[:, :, :], 0.0)
            nc.vector.memset(m.w2_s[:, :], 0.0)
            nc.vector.memset(m.zeros[:, :], 0.0).then_inc(s_const, 1)
            nc.vector.memset(ig["src"][:, (GC - 1) * GE:GC * GE], PAD_NODE).then_inc(s_pad, 1)
            nc.vector.memset(ig["dst"][:, (GC - 1) * GE:GC * GE], PAD_NODE).then_inc(s_pad, 1)
            nc.vector.memset(m.half[:, :], 0.5)
            nc.vector.memset(m.ones[:, :], 1.0).then_inc(s_const, 1)
            nc.vector.memset(m.split[:, :], 1.0).then_inc(s_const, 1)
            dve.wait_ge(s_const, 3)
            nc.vector.memset(m.split[0:1, :], float(P)).then_inc(s_const, 1)
            for a, name in enumerate(("src", "dst")):
                dve.wait_ge(s_idx[name], 48)
                nc.vector.tensor_copy(fg[name], ig[name]).then_inc(s_fg, 1)
            dve.wait_ge(s_fg, 2)
            v = fg["dst"].rearrange("p (c e) -> p c e", c=GC)
            nc.vector.tensor_reduce(lim[:, 0:GC], v, AX.X, ALU.min).then_inc(s_lim, 1)
            nc.vector.tensor_reduce(lim[:, GC:2 * GC], v, AX.X, ALU.max).then_inc(s_lim, 1)
            dve.wait_ge(s_lim, 2)
            nc.vector.tensor_tensor(lim[:, 2 * GC:3 * GC], lim[:, GC:2 * GC], lim[:, 0:GC],
                                    ALU.subtract).then_inc(s_lim, 1)
            dve.wait_ge(s_lim, 3)
            nc.vector.tensor_reduce(lim[:, 3 * GC:3 * GC + 1], lim[:, 2 * GC:3 * GC], AX.X, ALU.max).then_inc(s_lim, 1)
            n = 0
            for name in ("src", "dst"):
                o = cols[name].rearrange("p (g j) -> p j g", j=J)
                for c in range(GC):
                    ng = P if (c + 1) * P <= GPAD else GPAD - c * P
                    for jh in range(2):
                        dve.wait_ge(s_cols, n + 1)
                        nc.vector.tensor_copy(o[:, 4 * jh:4 * jh + 4, c * P:c * P + ng],
                                              psC[n % 2].rearrange("p (j g) -> p j g", j=4)[:, :, 0:ng]).then_inc(s_colsdone, 1)
                        n += 1
            dve.wait_ge(s_pool, 6)
            dve.wait_ge(s_colsdone, n)
            nc.vector.tensor_scalar(m.srcT[:, :], m.srcF[:, :], m.trash[:, 0:1], None, ALU.subtract).then_inc(s_srcT, 1)
            for n in range(2 * GC):
                name, c = ("src", "dst")[n // GC], n % GC
                piece = ig[name][:, c * GE:(c + 1) * GE]
                if n >= 1:
                    dve.wait_ge(s_hl, n)
                nc.vector.tensor_scalar(hi_i, piece, 7, None, ALU.logical_shift_right).then_inc(s_int, 1)
                nc.vector.tensor_scalar(lo_i, piece, P - 1, None, ALU.bitwise_and).then_inc(s_int, 1)
                dve.wait_ge(s_int, 2 * n + 2)
                if n >= 2:
                    dve.wait_ge(s_hlst[n % 2], 16 * (n // 2))
                nc.vector.tensor_copy(hl[n % 2][:, 0, :], hi_i)
                nc.vector.tensor_copy(hl[n % 2][:, 1, :], lo_i).then_inc(s_hl, 1)
            dve.wait_ge(s_limT, 2)
            nc.vector.tensor_copy(m.base_bc[:, :], psM).then_inc(s_bc, 1)
            nc.vector.tensor_copy(m.base_i[:, :], psM[0:1, :]).then_inc(s_bc, 1)
            nc.vector.tensor_scalar(work[:, 5950:5951], m.trash[:, 0:1], float(TRASH), None, ALU.subtract).then_inc(s_bc, 1)
            dve.wait_ge(s_bc, 3)
            nc.vector.tensor_scalar(m.winid[:, :], m.base_bc[:, :], work[:, 5950:5951], None, ALU.add).then_inc(s_bc, 1)
            nc.vector.tensor_reduce(flag_f, psS[0:1, 0:P], AX.X, ALU.max).then_inc(s_fl, 1)
            dve.wait_ge(s_fl, 1)
            nc.vector.tensor_scalar(m.flag_i[:, :], flag_f, float(P), None, ALU.is_lt).then_inc(s_fl, 1)
            dve.sem_inc(s_hb, 2)
            dve.sem_inc(s_hst[0], 32)
            dve.sem_inc(s_hst[1], 32)
            def bias(q, s, turn):
                dve.wait_ge(s_h, ready(q, 2))
                dve.wait_ge(s_hst[s], 16 * turn + 32)
                nc.vector.tensor_tensor(hb[s].rearrange("p (t f) -> p t f", t=B),
                                        psH[s].rearrange("p (t f) -> p t f", t=B),
                                        m.bin_s[0:NP, :].unsqueeze(1).to_broadcast([NP, B, F]), ALU.add).then_inc(s_hb, 1)
            over(dve, NB, bias)


def filter_layer(nc, m, io):
    ps, work = m.ps, m.work

    def slots(at, width, n=2):
        return [work[:, at + width * s:at + width * s + width] for s in range(n)]

    attr = slots(0, J * R)
    weight = slots(512, J)
    srow = [v[0:2, :].bitcast(BF16) for v in slots(544, GE // 2)]
    drow = [v[0:2, :].bitcast(BF16) for v in slots(1568, GE // 2)]
    hwin = slots(2592, F)
    attrT = work[:, 2720:2976]
    log1p = work[:, 2976:3488]
    relu = work[:, 3488:4000]
    hid = slots(4000, 512)
    pick = slots(5024, J * P)
    same = slots(7072, J * P)
    weighed = work[:, 9120:9632]
    msg = slots(9632, J * F)
    summed = slots(10656, J * F)
    sidx = [v.bitcast(U32) for v in slots(11680, J)]
    earlier = slots(11696, J)
    first = work[:, 11712:11712 + J]
    count = slots(11720, 2)
    gidx = [v.bitcast(U32) for v in slots(11730, J)]
    grow = slots(5024, J * F)
    one_lo = work[:, 6048:6560].bitcast(BF16)
    one_hi = work[:, 6560:6560 + 396].bitcast(BF16)
    dst_i = work[:, 2592:2592 + J].bitcast(I32)
    lo_i = work[:, 2600:2600 + J].bitcast(I32)
    hi_i = work[:, 2608:2608 + J].bitcast(I32)
    lo_f = work[:, 2616:2616 + J]
    hi_f = work[:, 2624:2624 + J]
    NHI = NT // P
    deg_hl = work[0:NHI, 9120:9120 + P]
    degrow = m.arena[0:1, :]

    ps_attr = ps[:, 1, 0:2 * P]
    ps_deg = ps[0:1, 0, 0:P]
    ps_hid = ps[:, 1, :]
    ps_filt = ps[:, 2, :]
    ps_row = ps[:, 3, :]
    ps_sum = ps[:, 4, :]
    ps_src = ps[:, 5:7, :].rearrange("p a b -> p (a b)")
    ps_dst = ps[:, 7, :]

    with ExitStack() as ctx:
        def sem(name):
            return ctx.enter_context(nc.semaphore(name))
        loaded = [sem("group_loaded0"), sem("group_loaded1")]
        gathered = [sem("rows_gathered0"), sem("rows_gathered1")]
        attr_turned, attr_copied, hid_made, ln_made, hid_done = (
            sem("attr_turned"), sem("attr_copied"), sem("hid_made"), sem("ln_made"), sem("hid_done"))
        act_steps = sem("act_steps")
        src_out, dst_out, same_done, pick_done = (
            sem("src_broadcast"), sem("dst_broadcast"), sem("same_done"), sem("pick_done"))
        filt_made, row_picked, weighed_done, msg_done = (
            sem("filter_made"), sem("rows_picked"), sem("weighed_done"), sem("msg_done"))
        sum_made, sum_copied, first_done, idx_done = (
            sem("sum_made"), sem("sum_copied"), sem("first_done"), sem("idx_done"))
        deg_turned, deg_added, gidx_done, pool_turn = (
            sem("deg_turned"), sem("deg_added"), sem("gidx_done"), sem("pool_turn"))
        digits, onehots, deg_counted, deg_stored = (
            sem("dst_digits"), sem("onehots_done"), sem("deg_counted"), sem("deg_stored"))
        deg_final = sem("deg_final")
        block = ctx.enter_context(nc.Block())

        def load(sp, g, s, turn, windows, last=False):
            at = E - GE if last else g * GE
            sp.dma_start(attr[s], io["edge_attr"][bass.ds(at, GE), :].rearrange("(p j) r -> p (j r)", p=P)).then_inc(loaded[s], 16)
            sp.dma_start(weight[s], io["edge_weight"][bass.ds(at, GE)].rearrange("(p j) -> p j", p=P)).then_inc(loaded[s], 16)
            sp.dma_start(srow[s], m.src_hl[bass.ds(g, 1), :, :].rearrange("o t e -> (o t) e")).then_inc(loaded[s], 16)
            if windows:
                sp.dma_start(drow[s], m.dst_hl[bass.ds(g, 1), :, :].rearrange("o t e -> (o t) e")).then_inc(loaded[s], 16)
                base = sp.value_load(m.base_i[0:1, bass.ds(g, 1)], min_val=0, max_val=N)
                sp.dma_start(hwin[s], m.h_tab[bass.ds(base, P), :]).then_inc(loaded[s], 16)

        def loads(windows):
            return 16 * (5 if windows else 3)

        def sync_way(sp, windows):
            load(sp, 0, 0, 0, windows)
            load(sp, 1, 1, 0, windows)
            with sp.Fori(0, (G - 3) // 2) as i:
                for s in range(2):
                    sp.wait_ge(msg_done, 2 * i + s + 2)
                    load(sp, 2 * i + s + 2, s, i + 1, windows)
            sp.wait_ge(msg_done, G - 3 + 2)
            load(sp, G - 1, 0, 0, windows, last=True)

        @block.sync
        def _(sp):
            flag = sp.value_load(m.flag_i[0:1, 0:1], min_val=0, max_val=1)
            with sp.If(flag == 1):
                sync_way(sp, True)
                sp.wait_ge(deg_final, 1)
                sp.dma_start(m.deg_tab.rearrange("(o n) -> o n", o=1), degrow).then_inc(deg_stored, 16)
            with sp.Else():
                sync_way(sp, False)
                sp.wait_ge(deg_final, 1)
                sp.dma_start(m.deg_tab.rearrange("(h l) -> h l", l=P), deg_hl).then_inc(deg_stored, 16)
            sp.wait_ge(deg_stored, 16)

        def pe_front_a(pe, g, s, turn, windows):
            pe.wait_ge(loaded[s], loads(windows) * (turn + 1))
            pe.wait_ge(ln_made, free(g))
            for q in range(2):
                t = pe.transpose(ps_attr[:, P * q:P * q + P], attr[s][:, P * q:P * q + P], m.ident[:, :])
            t.then_inc(attr_turned, 1)
            if windows:
                pick_half(pe, g, s, 0)
            pe.wait_ge(same_done, free(g))
            for q in range(2):
                mm = pe.matmul(ps_src[:, 512 * q:512 * q + 512], m.split[:, :], srow[s][:, 512 * q:512 * q + 512],
                               start=True, stop=True)
            mm.then_inc(src_out, 1)

        def pick_half(pe, g, s, q):
            pe.wait_ge(pick_done, 2 * g + q + 1)
            pe.matmul(ps_dst, m.split[:, :], drow[s][:, 512 * q:512 * q + 512], start=True, stop=True).then_inc(dst_out, 1)

        def pe_front_b(pe, g, s, turn, windows):
            pe.wait_ge(attr_copied, ready(g, 1))
            for q in range(4):
                mm = pe.matmul(ps_hid[:, P * q:P * q + P], m.w1_s[:, q % 2, :], attrT[:, P * (q // 2):P * (q // 2) + P],
                               start=True, stop=True)
            mm.then_inc(hid_made, 1)
            if windows:
                pick_half(pe, g, s, 1)

        def pe_back_a(pe, g, s, turn, windows):
            pe.wait_ge(hid_done, ready(g, 1))
            pe.wait_ge(weighed_done, free(g))
            pe.matmul(ps_filt, m.ones[:, :], m.b2_s[:, :], start=True, stop=False, skip_group_check=True)
            for q in range(J // 2):
                mm = pe.matmul(ps_filt[:, P * q:P * q + P], hid[s][:, P * q:P * q + P], m.w2_s[:, :],
                               start=False, stop=(q == J // 2 - 1), skip_group_check=True)
            mm.then_inc(filt_made, 1)
            if windows:
                pe.wait_ge(pick_done, 2 * g + 3)
                pe.wait_ge(deg_added, free(g))
                for q in range(2):
                    mm = pe.matmul(ps_deg, count[s][:, q:q + 1], m.ident[:, :], start=(q == 0), stop=(q == 1))
                mm.then_inc(deg_turned, 1)
                pe.wait_ge(msg_done, free(g))
                for j in range(J):
                    mm = pe.matmul(ps_row[:, F * j:F * j + F], pick[s][:, P * j:P * j + P], hwin[s][:, :],
                                   start=True, stop=True)
                mm.then_inc(row_picked, 1)
            else:
                pe.wait_ge(onehots, ready(g, 0))
                for j in range(J):
                    mm = pe.matmul(ps_dst[0:NHI, 0:P], one_hi.rearrange("p (j h) -> p j h", j=J)[:, j, :],
                                   one_lo[:, P * j:P * j + P], start=False, stop=False, skip_group_check=True)
                mm.then_inc(deg_counted, 1)

        def pe_back_b(pe, g, s, turn, windows):
            pe.wait_ge(same_done, ready(g, 1))
            pe.wait_ge(msg_done, ready(g, 1))
            pe.wait_ge(sum_copied, free(g))
            for j in range(J):
                mm = pe.matmul(ps_sum[:, F * j:F * j + F], same[s][:, P * j:P * j + P], msg[s][:, F * j:F * j + F],
                               start=True, stop=True)
            mm.then_inc(sum_made, 1)

        def tensor_way(pe, windows):
            def first_(g, s, turn):
                pe_front_a(pe, g, s, turn, windows)
                pe_front_b(pe, g, s, turn, windows)

            def step(g, s, turn):
                n, ns, nturn = g + 1, 1 - s, turn + s
                pe_front_a(pe, n, ns, nturn, windows)
                pe_back_a(pe, g, s, turn, windows)
                pe_front_b(pe, n, ns, nturn, windows)
                pe_back_b(pe, g, s, turn, windows)

            def last(g, s, turn):
                pe_back_a(pe, g, s, turn, windows)
                pe_back_b(pe, g, s, turn, windows)
            pipelined(pe, G, first_, step, last)

        @block.tensor
        def _(pe):
            pe.sem_inc(sum_made, 2)
            pe.sem_inc(row_picked, 2)
            pe.sem_inc(filt_made, 2)
            pe.sem_inc(hid_made, 1)
            pe.sem_inc(deg_counted, 1)
            flag = pe.value_load(m.flag_i[0:1, 0:1], min_val=0, max_val=1)
            with pe.If(flag == 1):
                tensor_way(pe, True)
            with pe.Else():
                pe.matmul(ps_dst[0:NHI, 0:P], m.zeros[0:1, 0:NHI], m.zeros[0:1, 0:P], start=True, stop=False,
                          skip_group_check=True)
                tensor_way(pe, False)
            pe.wait_ge(attr_turned, G)

        def act_front(act, g, s, turn):
            act.wait_ge(attr_turned, ready(g, 0))
            act.wait_ge(hid_made, free(g))
            nc.scalar.copy(attrT, ps_attr).then_inc(attr_copied, 1)
            act.wait_ge(hid_made, ready(g, 1))
            act.wait_ge(hid_done, free(g))
            nc.scalar.activation(log1p, ps_hid, ACT.Abs, bias=m.b1_s[:, 0:1]).then_inc(act_steps, 1)
            nc.scalar.activation(relu, ps_hid, ACT.Relu, bias=m.b1_s[:, 0:1])
            act.wait_ge(act_steps, 2 * g + 1)
            nc.scalar.activation(log1p, log1p, ACT.Exp, scale=-1.0).then_inc(act_steps, 1)
            act.wait_ge(act_steps, 2 * g + 2)
            nc.scalar.activation(log1p, log1p, ACT.Ln, scale=0.5, bias=m.half[:, 0:1]).then_inc(ln_made, 1)

        def act_back(act, g, s, turn):
            act.wait_ge(sum_made, ready(g, 2))
            for k in range(K):
                act.wait_ge(m.agg_added[k], 32 * g + ZEROED - 32)
            nc.scalar.copy(summed[s], ps_sum).then_inc(sum_copied, 1)

        @block.scalar
        def _(act):
            act.sem_inc(attr_copied, 1)
            act.sem_inc(ln_made, 1)
            act.sem_inc(sum_copied, 1)

            def step(g, s, turn):
                act_front(act, g + 1, 1 - s, turn + s)
                act_back(act, g, s, turn)
            pipelined(act, G, lambda g, s, t: act_front(act, g, s, t), step, lambda g, s, t: act_back(act, g, s, t))

        def dve_pick(dve, g, s, q):
            if q == 0:
                dve.wait_ge(row_picked, free(g))
            dve.wait_ge(dst_out, 2 * g + q + 1)
            half = P // 2
            nc.vector.tensor_scalar(pick[s].rearrange("w (j e) -> w e j", j=J)[:, half * q:half * q + half, :],
                                    ps_dst.rearrange("w (e j) -> w e j", j=J), m.winid[:, bass.ds(g, 1)], 0.0,
                                    ALU.is_equal, ALU.add, accum_out=count[s][:, q:q + 1]).then_inc(pick_done, 1)

        def dve_onehots(dve, g, s):
            nc.vector.tensor_copy(dst_i, m.dstF[:, bass.ds(g * J, J)]).then_inc(digits, 1)
            dve.wait_ge(digits, 5 * g + 1)
            nc.vector.tensor_scalar(hi_i, dst_i, 7, None, ALU.logical_shift_right).then_inc(digits, 1)
            nc.vector.tensor_scalar(lo_i, dst_i, P - 1, None, ALU.bitwise_and).then_inc(digits, 1)
            dve.wait_ge(digits, 5 * g + 3)
            nc.vector.tensor_copy(hi_f, hi_i).then_inc(digits, 1)
            nc.vector.tensor_copy(lo_f, lo_i).then_inc(digits, 1)
            dve.wait_ge(digits, 5 * g + 5)
            dve.wait_ge(deg_counted, free(g))
            for one, width, digit in ((one_lo, P, lo_f), (one_hi, NHI, hi_f)):
                last = nc.vector.tensor_tensor(one.rearrange("p (j h) -> p j h", j=J),
                                               m.iota_w[:, 0:width].unsqueeze(1).to_broadcast([P, J, width]),
                                               digit.unsqueeze(2).to_broadcast([P, J, width]), ALU.is_equal)
            last.then_inc(onehots, 1)

        def dve_front_a(dve, g, s, turn, windows):
            if windows:
                dve_pick(dve, g, s, 0)
            else:
                if not isinstance(g, int):
                    dve.wait_ge(msg_done, g)
                nc.vector.tensor_copy(gidx[s], m.dstF[:, bass.ds(g * J, J)]).then_inc(gidx_done, 1)

        def dve_front_b(dve, g, s, turn, windows):
            dve.wait_ge(src_out, ready(g, 0))
            dve.wait_ge(sum_made, free(g))
            for j in range(J):
                mm = nc.vector.scalar_tensor_tensor(same[s][:, P * j:P * j + P], ps_src.rearrange("p (e j) -> p j e", j=J)[:, j, :],
                                                    m.srcF[:, bass.ds(g * J + j, 1)], m.below[:, :], ALU.is_equal, ALU.mult,
                                                    accum_out=earlier[s][:, j:j + 1])
            mm.then_inc(same_done, 1)
            if windows:
                dve_pick(dve, g, s, 1)
            else:
                dve_onehots(dve, g, s)
            dve.wait_ge(same_done, ready(g, 1))
            nc.vector.scalar_tensor_tensor(first, earlier[s], 1.0, m.srcT[:, bass.ds(g * J, J)], ALU.is_equal,
                                           ALU.mult).then_inc(first_done, 1)
            dve.wait_ge(first_done, ready(g, 0))
            for k in range(K):
                dve.wait_ge(m.agg_added[k], 32 * g + ZEROED - 32)
            nc.vector.tensor_scalar(sidx[s], first, m.trash[:, 0:1], None, ALU.add).then_inc(idx_done, 1)
            dve.wait_ge(ln_made, ready(g, 1))
            dve.wait_ge(filt_made, free(g))
            nc.vector.tensor_tensor(hid[s], relu, log1p, ALU.add).then_inc(hid_done, 1)

        def dve_back(dve, g, s, turn, windows):
            dve.wait_ge(filt_made, ready(g, 2))
            nc.vector.tensor_tensor(weighed.rearrange("p (j f) -> p j f", j=J), ps_filt.rearrange("p (j f) -> p j f", j=J),
                                    weight[s].unsqueeze(2).to_broadcast([P, J, F]), ALU.mult).then_inc(weighed_done, 1)
            dve.wait_ge(weighed_done, ready(g, 1))
            if windows:
                dve.wait_ge(row_picked, ready(g, 2))
                rows = ps_row
            else:
                dve.wait_ge(gathered[s], 128 * turn + 128)
                rows = grow[s]
            dve.wait_ge(sum_made, free(g))
            nc.vector.tensor_tensor(msg[s], rows, weighed, ALU.mult).then_inc(msg_done, 1)
            if windows:
                base = dve.value_load(m.base_i[0:1, bass.ds(g, 1)], min_val=0, max_val=N)
                dve.wait_ge(deg_turned, ready(g, 0))
                here = degrow[:, bass.ds(base, P)]
                nc.vector.tensor_tensor(here, here, ps_deg, ALU.add).then_inc(deg_added, 1)
                dve.wait_ge(deg_added, ready(g, 1))

        def vector_way(dve, windows):
            def first_(g, s, turn):
                dve_front_a(dve, g, s, turn, windows)
                dve_front_b(dve, g, s, turn, windows)

            def step(g, s, turn):
                n, ns, nturn = g + 1, 1 - s, turn + s
                dve_front_a(dve, n, ns, nturn, windows)
                dve_back(dve, g, s, turn, windows)
                dve_front_b(dve, n, ns, nturn, windows)
            pipelined(dve, G, first_, step, lambda g, s, t: dve_back(dve, g, s, t, windows))

        @block.vector
        def _(dve):
            dve.sem_inc(hid_done, 1)
            dve.sem_inc(same_done, 1)
            dve.sem_inc(pick_done, 1)
            dve.sem_inc(weighed_done, 1)
            dve.sem_inc(msg_done, 1)
            nc.vector.memset(degrow, 0.0).then_inc(deg_added, 1)
            dve.wait_ge(deg_added, 1)
            flag = dve.value_load(m.flag_i[0:1, 0:1], min_val=0, max_val=1)
            with dve.If(flag == 1):
                vector_way(dve, True)
                dve.sem_inc(deg_final, 1)
            with dve.Else():
                vector_way(dve, False)
                dve.wait_ge(deg_counted, ready(G - 1, 1))
                nc.vector.tensor_copy(deg_hl, ps_dst[0:NHI, 0:P]).then_inc(deg_final, 1)
            dve.wait_ge(deg_final, 1)

        def gather(pool, g, s, turn):
            pool.wait_ge(gidx_done, ready(g, 0))
            if not isinstance(g, int):
                pool.wait_ge(msg_done, g)
            pool.sem_inc(pool_turn, 1)
            for j in range(J):
                nc.gpsimd.indirect_dma_start(
                    out=grow[s][:, F * j:F * j + F], out_offset=None, in_=m.h_tab[:, :],
                    in_offset=bass.IndirectOffsetOnAxis(ap=gidx[s][:, j:j + 1], axis=0)).then_inc(gathered[s], 16)

        def scatter(pool, g, s, turn):
            pool.wait_ge(idx_done, ready(g, 0))
            pool.wait_ge(sum_copied, ready(g, 1))
            for j in range(J):
                k = j % K
                pool.wait_ge(m.agg_added[k], 32 * g + 16 * (j // K) + ZEROED)
                pool.sem_inc(pool_turn, 1)
                nc.gpsimd.indirect_dma_start(
                    out=m.agg_tab[k][:, :], out_offset=bass.IndirectOffsetOnAxis(ap=sidx[s][:, j:j + 1], axis=0),
                    in_=summed[s][:, F * j:F * j + F], in_offset=None,
                    compute_op=ALU.add).then_inc(m.agg_added[k], 16)

        @block.gpsimd
        def _(pool):
            flag = pool.value_load(m.flag_i[0:1, 0:1], min_val=0, max_val=1)
            with pool.If(flag == 1):
                over(pool, G, lambda g, s, turn: scatter(pool, g, s, turn))
            with pool.Else():
                def step(g, s, turn):
                    gather(pool, g + 1, 1 - s, turn + s)
                    scatter(pool, g, s, turn)
                pipelined(pool, G, lambda g, s, t: gather(pool, g, s, t), step, lambda g, s, t: scatter(pool, g, s, t))
            for k in range(K):
                pool.wait_ge(m.agg_added[k], 32 * G + ZEROED)


def layer_norm_stats(nc, dve, m, work_at, steps, waited, base, q, s, mv):
    dve.sem_inc(waited, 1)
    stats = m.work[0:NP, work_at:work_at + 6 * B].rearrange("p (t s) -> p t s", t=B)
    pair = m.work[0:NP, work_at + 6 * B:work_at + 8 * B].rearrange("p (t s) -> p t s", t=B)
    for t in range(B):
        last = nc.vector.bn_stats(stats[:, t, :], m.xs_flat[:, bass.ds(q * (B * D) + t * D, D)])
    last.then_inc(steps, 1)
    dve.wait_ge(steps, base + 1)
    dve.sem_inc(waited, 1)
    for t in range(B):
        last = nc.vector.bn_aggr(pair[:, t, :], stats[:, t, :])
    last.then_inc(steps, 1)
    dve.wait_ge(steps, base + 2)
    nc.vector.tensor_copy(mv[:, bass.ds(q * (2 * B), 2 * B)], pair.rearrange("p t s -> p (t s)")).then_inc(steps, 1)


def node_update(nc, m, io):
    ps, work = m.ps, m.work
    tabs = [work[0:NP, 1024 * s:1024 * s + K * B * F] for s in range(2)]
    agg = [work[0:NP, 2048 + 256 * s:2304 + 256 * s] for s in range(2)]
    aggT = [work[0:F, 2560 + 512 * s:2560 + 512 * s + BW] for s in range(2)]
    log1p = work[:, 3584:3584 + BW]
    relu = work[:, 4096:4096 + BW]
    hid = [work[:, 4608 + 512 * s:4608 + 512 * s + BW] for s in range(2)]
    LN_AT = 5632
    mv = work[0:NP, 5700:5700 + 2 * NC]
    rstd = work[0:NP, 5900:5900 + NC]
    var = work[0:NP, 6000:6000 + NC]
    xT = [work[:, 6144 + 512 * s:6144 + 512 * s + BW] for s in range(2)]
    yb = [work[0:NP, 7168 + 512 * s:7680 + 512 * s] for s in range(2)]
    xn = [work[0:NP, 8192 + 512 * s:8704 + 512 * s] for s in range(2)]
    ps_a = [ps[0:F, s, 0:BW] for s in range(2)]
    ps_h = [ps[:, 2 + s, 0:BW] for s in range(2)]
    ps_o = [ps[0:NP, 4 + s, :] for s in range(2)]
    ps_xT = [ps[:, s, 0:BW] for s in range(2)]
    ps_y = [ps[0:NP, 2 + s, :] for s in range(2)]
    ps_yT = [ps[:, 4 + s, 0:BW] for s in range(2)]
    rows = m.arena[:, 0:N].rearrange("f (p c) -> f c p", c=NC)

    with ExitStack() as ctx:
        def sem(name):
            return ctx.enter_context(nc.semaphore(name))
        deg_in, dinv_steps, dinv_act, dinv_stored = sem("deg_in"), sem("dinv_steps"), sem("dinv_act"), sem("dinv_stored")
        tabs_in = [sem("tables_in0"), sem("tables_in1")]
        y_stored = [sem("y_stored0"), sem("y_stored1")]
        agg_sum, agg_turned, agg_copied = sem("agg_summed"), sem("agg_turned"), sem("agg_copied")
        hid_made, act_steps, ln_made, hid_done = sem("hidden_made"), sem("act_order"), sem("hidden_ln"), sem("hidden_done")
        waited = sem("ln_waited")
        out_made, res_done, steps = sem("out_made"), sem("residual_done"), sem("ln_steps")
        var_done, std_done, rstd_done = sem("var_done"), sem("std_done"), sem("rstd_done")
        x_done, x_turned, xT_copied = sem("x_normed"), sem("x_turned"), sem("xT_copied")
        x_kept, x_seen = sem("x_kept"), sem("x_seen")
        y_made, y_scaled, y_turned, yT_copied = sem("y_made"), sem("y_scaled"), sem("y_turned"), sem("yT_copied")
        block = ctx.enter_context(nc.Block())

        @block.sync
        def _(sp):
            sp.dma_start(m.dinv[:, :], m.deg_tab[0:N].rearrange("(p c) -> p c", p=NP)).then_inc(deg_in, 16)

            def load(q, s, turn):
                sp.wait_ge(agg_sum, free(q))
                for k in range(K):
                    sp.dma_start(tabs[s][:, B * F * k:B * F * k + B * F],
                                 m.agg_tab[k][0:N, :].rearrange("(p c) d -> p (c d)", p=NP)[:, bass.ds(q * (B * F), B * F)]
                                 ).then_inc(tabs_in[s], 16)
            over(sp, NB, load)
            sp.wait_ge(dinv_steps, 2)
            sp.dma_start(m.dinv_tab.rearrange("(p c) -> p c", p=NP), m.dinv[:, :]).then_inc(dinv_stored, 16)

            def store(q, s, turn):
                sp.wait_ge(y_scaled, ready(q, 1))
                sp.dma_start(m.y_tab[0:N, :].rearrange("(p c) d -> p (c d)", p=NP)[:, bass.ds(q * (B * D), B * D)],
                             yb[s]).then_inc(y_stored[s], 16)
            over(sp, NB, store)
            sp.wait_ge(y_stored[0], 16 * (NB // 2 + 2))
            sp.wait_ge(y_stored[1], 16 * (NB // 2 + 1))
            sp.wait_ge(dinv_stored, 16)

        @block.tensor
        def _(pe):
            pe.sem_inc(agg_turned, 2)
            pe.sem_inc(hid_made, 2)
            pe.sem_inc(out_made, 2)

            def turn_agg(q, s):
                pe.wait_ge(agg_sum, ready(q, 2))
                pe.wait_ge(agg_copied, free(q))
                for t in range(B):
                    tr = pe.matmul(ps_a[s][:, NP * t:NP * t + NP], agg[s][:, F * t:F * t + F], m.ident[0:NP, 0:NP],
                                   start=True, stop=True)
                tr.then_inc(agg_turned, 1)

            def hidden(q, s):
                pe.wait_ge(agg_copied, ready(q, 2))
                pe.wait_ge(ln_made, free(q))
                pe.matmul(ps_h[s], m.wo1_s[:, :], aggT[s], start=True, stop=True).then_inc(hid_made, 1)

            def output(q, s):
                pe.wait_ge(hid_done, ready(q, 1))
                pe.wait_ge(res_done, free(q))
                pe.matmul(ps_o[s], m.ones[:, 0:NP], m.bo2_s[:, :], start=True, stop=False, skip_group_check=True)
                for t in range(B):
                    mm = pe.matmul(ps_o[s][:, D * t:D * t + D], hid[s][:, NP * t:NP * t + NP], m.wo2_s[:, :],
                                   start=False, stop=(t == B - 1), skip_group_check=True)
                mm.then_inc(out_made, 1)

            def first(q, s, turn):
                turn_agg(q, s)
                hidden(q, s)

            def step(q, s, turn):
                turn_agg(q + 1, 1 - s)
                hidden(q + 1, 1 - s)
                output(q, s)
            pipelined(pe, NB, first, step, lambda q, s, turn: output(q, s))

            pe.sem_inc(x_turned, 2)
            pe.sem_inc(y_made, 2)
            pe.sem_inc(y_turned, 2)

            def turn_x(q, s):
                pe.wait_ge(x_done, ready(q, 0))
                pe.wait_ge(xT_copied, free(q))
                for t in range(B):
                    tr = pe.transpose(ps_xT[s][:, NP * t:NP * t + NP], xn[s][:, D * t:D * t + D],
                                      m.ident[0:NP, 0:NP])
                tr.then_inc(x_turned, 1)

            def times_w(q, s):
                pe.wait_ge(xT_copied, ready(q, 2))
                if not isinstance(q, int):
                    pe.wait_ge(y_scaled, q)
                for t in range(B):
                    mm = pe.matmul(ps_y[s][:, D * t:D * t + D], xT[s][:, NP * t:NP * t + NP], m.W_s[:, :],
                                   start=True, stop=True)
                mm.then_inc(y_made, 1)

            def turn_y(q, s):
                pe.wait_ge(y_scaled, ready(q, 1))
                pe.wait_ge(yT_copied, free(q))
                for t in range(B):
                    tr = pe.transpose(ps_yT[s][:, NP * t:NP * t + NP], yb[s][:, D * t:D * t + D], m.ident[0:NP, 0:NP])
                tr.then_inc(y_turned, 1)

            def first_y(q, s, turn):
                turn_x(q, s)
                times_w(q, s)

            def step_y(q, s, turn):
                turn_x(q + 1, 1 - s)
                times_w(q + 1, 1 - s)
                turn_y(q, s)
            pipelined(pe, NB, first_y, step_y, lambda q, s, turn: turn_y(q, s))

        @block.gpsimd
        def _(pool):
            pool.sem_inc(x_kept, 2)

            def keep(q, s, turn):
                pool.wait_ge(x_done, ready(q, 0))
                pool.sem_inc(x_seen, 1)
                nc.gpsimd.tensor_copy(m.xs_flat[:, bass.ds(q * (B * D), B * D)], xn[s]).then_inc(x_kept, 1)
            over(pool, NB, keep)

        @block.scalar
        def _(act):
            act.wait_ge(dinv_steps, 1)
            nc.scalar.activation(m.dinv[:, :], m.dinv[:, :], ACT.Sqrt).then_inc(dinv_act, 1)
            act.sem_inc(agg_copied, 2)
            act.sem_inc(ln_made, 2)

            def step(q, s, turn):
                act.wait_ge(agg_turned, ready(q, 2))
                act.wait_ge(hid_made, free(q))
                nc.scalar.copy(aggT[s], ps_a[s]).then_inc(agg_copied, 1)
                act.wait_ge(hid_made, ready(q, 2))
                act.wait_ge(hid_done, free(q))
                nc.scalar.activation(log1p, ps_h[s], ACT.Abs, bias=m.bo1_s[:, 0:1]).then_inc(act_steps, 1)
                nc.scalar.activation(relu, ps_h[s], ACT.Relu, bias=m.bo1_s[:, 0:1])
                act.wait_ge(act_steps, 2 * q + 1)
                nc.scalar.activation(log1p, log1p, ACT.Exp, scale=-1.0).then_inc(act_steps, 1)
                act.wait_ge(act_steps, 2 * q + 2)
                nc.scalar.activation(log1p, log1p, ACT.Ln, scale=0.5, bias=m.half[:, 0:1]).then_inc(ln_made, 1)
            over(act, NB, step)

            act.wait_ge(var_done, 1)
            nc.scalar.activation(rstd, var, ACT.Sqrt).then_inc(std_done, 1)
            act.sem_inc(xT_copied, 2)
            act.sem_inc(y_scaled, 1)
            act.sem_inc(y_stored[0], 16)
            act.sem_inc(y_stored[1], 16)
            act.wait_ge(dinv_steps, 2)

            def step_y(q, s, turn):
                act.wait_ge(x_turned, ready(q, 2))
                act.wait_ge(y_made, free(q))
                nc.scalar.copy(xT[s], ps_xT[s]).then_inc(xT_copied, 1)
                act.wait_ge(y_made, ready(q, 2))
                act.wait_ge(y_stored[s], 16 * turn + 16)
                act.wait_ge(y_turned, free(q))
                for t in range(B):
                    last = nc.scalar.activation(yb[s][:, D * t:D * t + D], ps_y[s][:, D * t:D * t + D], ACT.Copy,
                                                scale=m.dinv[:, bass.ds(q * B + t, 1)])
                last.then_inc(y_scaled, 1)
            over(act, NB, step_y)

        @block.vector
        def _(dve):
            dve.sem_inc(agg_sum, 2)
            dve.sem_inc(hid_done, 1)
            dve.sem_inc(res_done, 2)
            dve.wait_ge(deg_in, 16)
            nc.vector.tensor_scalar(m.dinv[:, :], m.dinv[:, :], 1.0, None, ALU.add).then_inc(dinv_steps, 1)
            nc.vector.memset(m.arena[:, N:NT], 0.0)
            dve.wait_ge(dinv_act, 1)
            nc.vector.reciprocal(m.dinv[:, :], m.dinv[:, :]).then_inc(dinv_steps, 1)

            def sum_tables(q, s, turn):
                dve.wait_ge(tabs_in[s], 16 * K * (turn + 1))
                dve.wait_ge(agg_turned, free(q))
                nc.vector.tensor_reduce(agg[s], tabs[s].rearrange("p (k n) -> p n k", k=K), AX.X,
                                        ALU.add).then_inc(agg_sum, 1)

            def add_hidden(q, s, turn):
                dve.wait_ge(ln_made, ready(q, 2))
                dve.wait_ge(out_made, free(q))
                nc.vector.tensor_tensor(hid[s], relu, log1p, ALU.add).then_inc(hid_done, 1)

            def residual(q, s, turn):
                dve.wait_ge(out_made, ready(q, 2))
                here = m.xs_flat[:, bass.ds(q * (B * D), B * D)]
                nc.vector.tensor_tensor(here, here, ps_o[s], ALU.add).then_inc(res_done, 1)
                dve.wait_ge(res_done, ready(q, 2))
                layer_norm_stats(nc, dve, m, LN_AT, steps, waited, 3 * q, q, s, mv)

            def first(q, s, turn):
                sum_tables(q, s, turn)
                add_hidden(q, s, turn)

            def step(q, s, turn):
                sum_tables(q + 1, 1 - s, turn + s)
                add_hidden(q + 1, 1 - s, turn + s)
                residual(q, s, turn)
            pipelined(dve, NB, first, step, residual)
            dve.wait_ge(steps, 3 * NB)
            mvv = mv.rearrange("p (c s) -> p c s", s=2)
            nc.vector.tensor_scalar(var, mvv[:, :, 1], LN_EPS, None, ALU.add).then_inc(var_done, 1)
            dve.wait_ge(std_done, 1)
            nc.vector.reciprocal(rstd, rstd).then_inc(rstd_done, 1)
            dve.wait_ge(rstd_done, 1)
            dve.sem_inc(yT_copied, 2)

            def norm(q, s, turn):
                dve.wait_ge(x_kept, free(q))
                dve.wait_ge(x_turned, free(q))
                for t in range(B):
                    here = m.xs_flat[:, bass.ds(q * (B * D) + t * D, D)]
                    last = nc.vector.tensor_scalar(xn[s][:, D * t:D * t + D], here, mv[:, bass.ds(q * (2 * B) + 2 * t, 1)],
                                                   rstd[:, bass.ds(q * B + t, 1)], ALU.subtract, ALU.mult)
                last.then_inc(x_done, 1)

            def keep_yT(q, s, turn):
                dve.wait_ge(y_turned, ready(q, 2))
                nc.vector.tensor_copy(rows[:, bass.ds(q * B, B), :], ps_yT[s].rearrange("f (t p) -> f t p", t=B)).then_inc(yT_copied, 1)

            def step_y(q, s, turn):
                norm(q + 1, 1 - s, turn)
                keep_yT(q, s, turn)
            pipelined(dve, NB, norm, step_y, keep_yT)


def graph_layer(nc, m, io):
    ps, work = m.ps, m.work

    def slots(at, width):
        return [work[:, at + width * s:at + width * s + width] for s in range(2)]

    grow = slots(0, J * D)
    pick = slots(2048, J * P)
    gidx = [v.bitcast(U32) for v in slots(4096, J)]
    place = slots(4112, J)
    drow = [v[0:2, :].bitcast(BF16) for v in slots(4160, GE // 2)]
    same = slots(2048, J * P)
    summed = slots(5200, J * D)
    sidx = [v.bitcast(U32) for v in slots(7250, J)]
    earlier = slots(7270, J)
    first = work[:, 7290:7290 + J]
    dstT = work[:, 7300:7300 + J]
    tabs = work[0:NP, 7400:7400 + K * B * D]
    total = work[0:NP, 9448:9448 + B * D]
    ps_win = [ps[:, s, 0:P] for s in range(2)]
    ps_sum = ps[:, 2:4, :].rearrange("p a b -> p (a b)")
    ps_dst = ps[:, 4:6, :].rearrange("p a b -> p (a b)")
    ps_tot = ps[:, 6, 0:BW]
    rows = m.arena[:, 0:N].rearrange("f (p c) -> f c p", c=NC)

    with ExitStack() as ctx:
        def sem(name):
            return ctx.enter_context(nc.semaphore(name))
        gathered = [sem("y_gathered0"), sem("y_gathered1")]
        loaded = [sem("dst_loaded0"), sem("dst_loaded1")]
        gidx_done, place_done, pick_done = sem("y_idx_done"), sem("place_done"), sem("y_pick_done")
        win_made, win_added, pool_turn = sem("window_made"), sem("window_added"), sem("y_pool_turn")
        dst_out, same_done, first_done, idx_done = sem("dst_out"), sem("y_same"), sem("y_first"), sem("y_sidx")
        sum_made, sum_copied, dstT_done = sem("y_sum_made"), sem("y_sum_copied"), sem("dstT_done")
        tabs_in, tot_done, tot_turned, tot_added = sem("y_tabs_in"), sem("tot_done"), sem("tot_turned"), sem("tot_added")
        all_added = sem("all_scattered")
        block = ctx.enter_context(nc.Block())

        def gather(pool, g, s, turn, used):
            pool.wait_ge(gidx_done, ready(g, 0))
            pool.wait_ge(used, free(g))
            pool.sem_inc(pool_turn, 1)
            for j in range(J):
                nc.gpsimd.indirect_dma_start(
                    out=grow[s][:, D * j:D * j + D], out_offset=None, in_=m.y_tab[:, :],
                    in_offset=bass.IndirectOffsetOnAxis(ap=gidx[s][:, j:j + 1], axis=0)).then_inc(gathered[s], 16)

        def scatter(pool, g, s, turn):
            pool.wait_ge(idx_done, ready(g, 0))
            pool.wait_ge(sum_copied, ready(g, 1))
            for j in range(J):
                k = j % K
                pool.wait_ge(m.out_added[k], 32 * g + 16 * (j // K) + ZEROED)
                pool.sem_inc(pool_turn, 1)
                nc.gpsimd.indirect_dma_start(
                    out=m.out_tab[k][:, :], out_offset=bass.IndirectOffsetOnAxis(ap=sidx[s][:, j:j + 1], axis=0),
                    in_=summed[s][:, D * j:D * j + D], in_offset=None,
                    compute_op=ALU.add).then_inc(m.out_added[k], 16)

        @block.gpsimd
        def _(pool):
            flag = pool.value_load(m.flag_i[0:1, 0:1], min_val=0, max_val=1)
            with pool.If(flag == 1):
                over(pool, G, lambda g, s, turn: gather(pool, g, s, turn, win_made))
            with pool.Else():
                for k in range(K):
                    zero_table(pool, m.out_tab[k], D, m.zeros, m.out_added[k])

                def step(g, s, turn):
                    gather(pool, g + 1, 1 - s, turn + s, sum_made)
                    scatter(pool, g, s, turn)
                pipelined(pool, G, lambda g, s, turn: gather(pool, g, s, turn, sum_made), step,
                          lambda g, s, turn: scatter(pool, g, s, turn))
                for k in range(K):
                    pool.wait_ge(m.out_added[k], 32 * G + ZEROED)
                pool.sem_inc(all_added, 1)
            pool.wait_ge(pool_turn, G)

        @block.tensor
        def _(pe):
            pe.sem_inc(win_made, 2)
            pe.sem_inc(sum_made, 2)
            flag = pe.value_load(m.flag_i[0:1, 0:1], min_val=0, max_val=1)
            with pe.If(flag == 1):
                def window(g, s, turn):
                    pe.wait_ge(gathered[s], 128 * turn + 128)
                    pe.wait_ge(pick_done, ready(g, 0))
                    pe.wait_ge(win_added, free(g))
                    for j in range(J):
                        mm = pe.matmul(ps_win[s], grow[s][:, D * j:D * j + D], pick[s][:, P * j:P * j + P],
                                       start=(j == 0), stop=(j == J - 1))
                    mm.then_inc(win_made, 1)
                over(pe, G, window)
            with pe.Else():
                def spread(g, s, turn):
                    pe.wait_ge(loaded[s], 16 * turn + 16)
                    pe.wait_ge(same_done, free(g))
                    for q in range(2):
                        mm = pe.matmul(ps_dst[:, 512 * q:512 * q + 512], m.split[:, :], drow[s][:, 512 * q:512 * q + 512],
                                       start=True, stop=True)
                    mm.then_inc(dst_out, 1)

                def sums(g, s, turn):
                    pe.wait_ge(same_done, ready(g, 1))
                    pe.wait_ge(gathered[s], 128 * turn + 128)
                    pe.wait_ge(sum_copied, free(g))
                    for j in range(J):
                        mm = pe.matmul(ps_sum[:, D * j:D * j + D], same[s][:, P * j:P * j + P], grow[s][:, D * j:D * j + D],
                                       start=True, stop=True)
                    mm.then_inc(sum_made, 1)

                def step(g, s, turn):
                    spread(g + 1, 1 - s, turn + s)
                    sums(g, s, turn)
                pipelined(pe, G, spread, step, sums)
                with pe.Fori(0, NB) as q:
                    pe.wait_ge(tot_done, q + 1)
                    for t in range(B):
                        tr = pe.transpose(ps_tot[:, NP * t:NP * t + NP], total[:, D * t:D * t + D], m.ident[0:NP, 0:NP])
                    tr.then_inc(tot_turned, 1)
            pe.wait_ge(gathered[0], 128)

        @block.sync
        def _(sp):
            flag = sp.value_load(m.flag_i[0:1, 0:1], min_val=0, max_val=1)
            with sp.If(flag == 0):
                def load(g, s, turn):
                    sp.wait_ge(same_done, g)
                    sp.dma_start(drow[s], m.dst_hl[bass.ds(g, 1), :, :].rearrange("o t e -> (o t) e")).then_inc(loaded[s], 16)
                sp.dma_start(drow[0], m.dst_hl[0, :, :]).then_inc(loaded[0], 16)
                sp.dma_start(drow[1], m.dst_hl[1, :, :]).then_inc(loaded[1], 16)
                with sp.Fori(0, (G - 3) // 2) as i:
                    load(2 * i + 2, 0, None)
                    load(2 * i + 3, 1, None)
                load(G - 1, 0, None)
                sp.wait_ge(all_added, 1)
                with sp.Fori(0, NB) as q:
                    sp.wait_ge(tot_added, q + 1)
                    for k in range(K):
                        sp.dma_start(tabs[:, B * D * k:B * D * k + B * D],
                                     m.out_tab[k][0:N, :].rearrange("(p c) d -> p (c d)", p=NP)[:, bass.ds(q * (B * D), B * D)]
                                     ).then_inc(tabs_in, 16)
            with sp.Else():
                sp.sem_inc(all_added, 1)
            sp.wait_ge(all_added, 1)

        @block.scalar
        def _(act):
            flag = act.value_load(m.flag_i[0:1, 0:1], min_val=0, max_val=1)
            with act.If(flag == 0):
                act.sem_inc(sum_copied, 1)

                def copy(g, s, turn):
                    act.wait_ge(sum_made, ready(g, 2))
                    for k in range(K):
                        act.wait_ge(m.out_added[k], 32 * g + ZEROED - 32)
                    nc.scalar.copy(summed[s], ps_sum).then_inc(sum_copied, 1)
                over(act, G, copy)
            with act.Else():
                act.sem_inc(all_added, 1)
            act.wait_ge(all_added, 1)

        def same_rows(dve, g, s):
            dve.wait_ge(dst_out, ready(g, 0))
            dve.wait_ge(sum_made, free(g))
            for j in range(J):
                mm = nc.vector.scalar_tensor_tensor(same[s][:, P * j:P * j + P], ps_dst.rearrange("p (e j) -> p j e", j=J)[:, j, :],
                                                    m.dstF[:, bass.ds(g * J + j, 1)], m.below[:, :], ALU.is_equal, ALU.mult,
                                                    accum_out=earlier[s][:, j:j + 1])
            mm.then_inc(same_done, 1)
            nc.vector.tensor_scalar(dstT, m.dstF[:, bass.ds(g * J, J)], m.trash[:, 0:1], None, ALU.subtract).then_inc(dstT_done, 1)
            dve.wait_ge(same_done, ready(g, 1))
            dve.wait_ge(dstT_done, ready(g, 0))
            nc.vector.scalar_tensor_tensor(first, earlier[s], 1.0, dstT, ALU.is_equal, ALU.mult).then_inc(first_done, 1)
            dve.wait_ge(first_done, ready(g, 0))
            for k in range(K):
                dve.wait_ge(m.out_added[k], 32 * g + ZEROED - 32)
            nc.vector.tensor_scalar(sidx[s], first, m.trash[:, 0:1], None, ALU.add).then_inc(idx_done, 1)

        def indices(dve, g, s, turn, used):
            dve.wait_ge(used, free(g))
            nc.vector.tensor_copy(gidx[s], m.srcF[:, bass.ds(g * J, J)]).then_inc(gidx_done, 1)

        @block.vector
        def _(dve):
            dve.sem_inc(win_added, 2)
            dve.sem_inc(same_done, 1)
            flag = dve.value_load(m.flag_i[0:1, 0:1], min_val=0, max_val=1)
            with dve.If(flag == 1):
                def front(g, s, turn):
                    indices(dve, g, s, turn, win_made)
                    nc.vector.tensor_scalar(place[s], m.dstF[:, bass.ds(g * J, J)], m.base_bc[:, bass.ds(g, 1)], None,
                                            ALU.subtract).then_inc(place_done, 1)
                    dve.wait_ge(place_done, ready(g, 0))
                    dve.wait_ge(win_made, free(g))
                    nc.vector.tensor_tensor(pick[s].rearrange("p (j w) -> p j w", j=J),
                                            m.iota_w[:, :].unsqueeze(1).to_broadcast([P, J, P]),
                                            place[s].unsqueeze(2).to_broadcast([P, J, P]), ALU.is_equal).then_inc(pick_done, 1)

                def back(g, s, turn):
                    base = dve.value_load(m.base_i[0:1, bass.ds(g, 1)], min_val=0, max_val=N)
                    dve.wait_ge(win_made, ready(g, 2))
                    here = m.arena[:, bass.ds(base, P)]
                    nc.vector.tensor_tensor(here, here, ps_win[s], ALU.add).then_inc(win_added, 1)
                    dve.wait_ge(win_added, ready(g, 2))

                def step(g, s, turn):
                    front(g + 1, 1 - s, turn + s)
                    back(g, s, turn)
                pipelined(dve, G, front, step, back)
            with dve.Else():
                def gfront(g, s, turn):
                    indices(dve, g, s, turn, sum_made)
                    same_rows(dve, g, s)
                over(dve, G, gfront)
                dve.sem_inc(tot_added, 1)
                with dve.Fori(0, NB) as q:
                    dve.wait_ge(tabs_in, q * (16 * K) + 16 * K)
                    nc.vector.tensor_reduce(total, tabs.rearrange("p (k n) -> p n k", k=K), AX.X, ALU.add).then_inc(tot_done, 1)
                    dve.wait_ge(tot_turned, q + 1)
                    here = rows[:, bass.ds(q * B, B), :]
                    nc.vector.tensor_tensor(here, here, ps_tot.rearrange("f (t p) -> f t p", t=B), ALU.add).then_inc(tot_added, 1)
            dve.wait_ge(gidx_done, G)


def norm_and_store(nc, m, io):
    ps, work = m.ps, m.work
    drow = [work[0:1, 512 * s:512 * s + BW] for s in range(2)]
    stats = work[:, 1024:1024 + 6 * NB]
    mean_var = work[:, 1200:1202]
    std, scale, shift = work[:, 1202:1203], work[:, 1203:1204], work[:, 1204:1205]
    var_eps, mean_scale = work[:, 1205:1206], work[:, 1206:1207]
    turned = [work[:, 1536 + 512 * s:1536 + 512 * s + BW] for s in range(2)]
    LN_AT = 2600
    mv = work[0:NP, 2700:2700 + 2 * NC]
    rstd = work[0:NP, 2900:2900 + NC]
    var = work[0:NP, 3000:3000 + NC]
    ps_d = [ps[:, s, 0:BW] for s in range(2)]
    ps_r = [ps[0:NP, 2 + s, :] for s in range(2)]
    rows = m.arena[:, 0:N].rearrange("f (p c) -> f c p", c=NC)
    with ExitStack() as ctx:
        def sem(name):
            return ctx.enter_context(nc.semaphore(name))
        row_in = [sem("dinv_row0"), sem("dinv_row1")]
        spread, scaled, bn_steps, bn_agg = sem("dinv_spread"), sem("sums_scaled"), sem("bn_steps"), sem("bn_aggregated")
        bn_std, bn_ready = sem("bn_std"), sem("bn_ready")
        relu_done, turned_back, res_done, steps = sem("relu_done"), sem("turned_back"), sem("residual2"), sem("ln2_steps")
        waited = sem("ln2_waited")
        var_done, std_done, rstd_done, x_done, stored = (
            sem("var2_done"), sem("std2_done"), sem("rstd2_done"), sem("x2_done"), sem("out_stored"))
        block = ctx.enter_context(nc.Block())

        @block.sync
        def _(sp):
            def load(q, s, turn):
                sp.wait_ge(spread, free(q))
                sp.dma_start(drow[s], m.dinv_tab[bass.ds(q * BW, BW)].rearrange("(o n) -> o n", o=1)).then_inc(row_in[s], 16)
            over(sp, NB, load)
            flat = io["out"].rearrange("(p c) d -> p (c d)", p=NP)
            with sp.Fori(0, NB) as q:
                sp.wait_ge(x_done, q + 1)
                sp.dma_start(flat[:, bass.ds(q * (B * D), B * D)], m.xs_flat[:, bass.ds(q * (B * D), B * D)]).then_inc(stored, 16)
            sp.wait_ge(stored, 16 * NB)

        @block.tensor
        def _(pe):
            pe.sem_inc(spread, 2)

            def row(q, s, turn):
                pe.wait_ge(row_in[s], 16 * turn + 16)
                pe.wait_ge(scaled, free(q))
                pe.matmul(ps_d[s], m.ones[:, :], drow[s], start=True, stop=True).then_inc(spread, 1)
            over(pe, NB, row)
            pe.sem_inc(turned_back, 2)

            def back(q, s, turn):
                pe.wait_ge(relu_done, ready(q, 0))
                pe.wait_ge(res_done, free(q))
                for t in range(B):
                    tr = pe.transpose(ps_r[s][:, D * t:D * t + D], turned[s][:, NP * t:NP * t + NP], m.ident[:, :])
                tr.then_inc(turned_back, 1)
            over(pe, NB, back)

        @block.scalar
        def _(act):
            act.wait_ge(bn_agg, 2)
            nc.scalar.activation(std, var_eps, ACT.Sqrt).then_inc(bn_std, 1)
            act.wait_ge(bn_ready, 4)

            def normed(q, s, turn):
                act.wait_ge(turned_back, free(q))
                nc.scalar.activation(turned[s].rearrange("f (t p) -> f t p", t=B), rows[:, bass.ds(q * B, B), :], ACT.Relu,
                                     bias=shift, scale=scale).then_inc(relu_done, 1)
            over(act, NB, normed)
            act.wait_ge(var_done, 1)
            nc.scalar.activation(rstd, var, ACT.Sqrt).then_inc(std_done, 1)

        @block.vector
        def _(dve):
            dve.sem_inc(scaled, 2)

            def scale_sums(q, s, turn):
                here = m.arena[:, bass.ds(q * BW, BW)]
                dve.wait_ge(spread, ready(q, 2))
                nc.vector.tensor_tensor(here, here, ps_d[s], ALU.mult).then_inc(scaled, 1)
                dve.wait_ge(scaled, ready(q, 2))
                nc.vector.tensor_scalar(here, here, m.gbb[:, 0:1], None, ALU.add).then_inc(bn_steps, 1)
                dve.wait_ge(bn_steps, 2 * q + 1)
                dve.sem_inc(waited, 1)
                nc.vector.bn_stats(stats[:, bass.ds(q * 6, 6)], here).then_inc(bn_steps, 1)
            over(dve, NB, scale_sums)
            dve.wait_ge(bn_steps, 2 * NB)
            nc.vector.bn_aggr(mean_var, stats).then_inc(bn_agg, 1)
            dve.wait_ge(bn_agg, 1)
            nc.vector.tensor_scalar(var_eps, mean_var[:, 1:2], BN_EPS, None, ALU.add).then_inc(bn_agg, 1)
            dve.wait_ge(bn_std, 1)
            nc.vector.reciprocal(std, std).then_inc(bn_ready, 1)
            dve.wait_ge(bn_ready, 1)
            nc.vector.tensor_tensor(scale, std, m.gbb[:, 1:2], ALU.mult).then_inc(bn_ready, 1)
            dve.wait_ge(bn_ready, 2)
            nc.vector.tensor_tensor(mean_scale, mean_var[:, 0:1], scale, ALU.mult).then_inc(bn_ready, 1)
            dve.wait_ge(bn_ready, 3)
            nc.vector.tensor_tensor(shift, m.gbb[:, 2:3], mean_scale, ALU.subtract).then_inc(bn_ready, 1)
            dve.sem_inc(res_done, 2)

            def residual(q, s, turn):
                dve.wait_ge(turned_back, ready(q, 2))
                here = m.xs_flat[:, bass.ds(q * (B * D), B * D)]
                nc.vector.tensor_tensor(here, here, ps_r[s], ALU.add).then_inc(res_done, 1)
                dve.wait_ge(res_done, ready(q, 2))
                layer_norm_stats(nc, dve, m, LN_AT, steps, waited, 3 * q, q, s, mv)
            over(dve, NB, residual)
            dve.wait_ge(steps, 3 * NB)
            nc.vector.tensor_scalar(var, mv.rearrange("p (c s) -> p c s", s=2)[:, :, 1], LN_EPS, None, ALU.add).then_inc(var_done, 1)
            dve.wait_ge(std_done, 1)
            nc.vector.reciprocal(rstd, rstd).then_inc(rstd_done, 1)
            dve.wait_ge(rstd_done, 1)
            with dve.Fori(0, NB) as q:
                for t in range(B):
                    here = m.xs_flat[:, bass.ds(q * (B * D) + t * D, D)]
                    last = nc.vector.tensor_scalar(here, here, mv[:, bass.ds(q * (2 * B) + 2 * t, 1)],
                                                   rstd[:, bass.ds(q * B + t, 1)], ALU.subtract, ALU.mult)
                last.then_inc(x_done, 1)


def program(nc, io):
    with ExitStack() as ctx:
        m = Memory(nc, ctx)
        setup(nc, m, io)
        filter_layer(nc, m, io)
        node_update(nc, m, io)
        graph_layer(nc, m, io)
        norm_and_store(nc, m, io)


def kernel(**inputs):
    import numpy as np
    import concourse.bacc as bacc
    from concourse.bass_utils import run_bass_kernel_spmd

    nc = bacc.Bacc("TRN2", target_bir_lowering=False, num_devices=1)
    arrays, io = {}, {}
    for name, given in INPUTS.items():
        a = np.ascontiguousarray(inputs[given])
        arrays[f"in_{name}"] = a
        io[name] = nc.dram_tensor(f"in_{name}", a.shape, mybir.dt.from_np(a.dtype), kind="ExternalInput").ap()
    io["out"] = nc.dram_tensor("out", (N, D), F32, kind="ExternalOutput").ap()
    program(nc, io)
    r = run_bass_kernel_spmd(nc, [arrays], core_ids=[0])
    return r.results[0]["out"]
```

```python
from contextlib import ExitStack

import concourse.bass as bass
from concourse import mybir

F32 = mybir.dt.float32
BF16 = mybir.dt.bfloat16
I32 = mybir.dt.int32
U32 = mybir.dt.uint32
ALU = mybir.AluOpType
ACT = mybir.ActivationFunctionType
AX = mybir.AxisListType

P = 128
N, E = 12500, 412500
D, F, R = 128, 64, 32
J = 8
GE = J * P
G = -(-E // GE)
SEEN = G * GE - E
GC = -(-G // P)
GPAD = 416
PAD_NODE = N
TRASH = N + 1
NT = 99 * P
K = 4
NP, NC = 125, 100
B = 4
NB = NC // B
BW = B * NP
LN_EPS = BN_EPS = 1e-5
ZERO_COLS = 1056
ZEROED = 48
WORK = 11808


def ready(g, depth):
    return g + 1 + depth


def free(g):
    return g + 1


def over(eng, n, body):
    with eng.Fori(0, n // 2) as i:
        body(2 * i, 0, i)
        body(2 * i + 1, 1, i)
    if n % 2:
        body(n - 1, 0, n // 2)


def pipelined(eng, n, first, step, last):
    first(0, 0, 0)
    with eng.Fori(0, n // 2) as i:
        step(2 * i, 0, i)
        step(2 * i + 1, 1, i)
    last(n - 1, 0, n // 2)


def staged(eng, stage):
    def near(g):
        return [(k, k % 2, k // 2) if 0 <= k < G else None for k in (g - 1, g, g + 1)]
    stage(*near(-1))
    stage(*near(0))
    with eng.Fori(0, (G - 3) // 2) as i:
        for g in (1, 2):
            stage(*[(2 * i + k, k % 2, i + k // 2) for k in (g - 1, g, g + 1)])
    for g in (G - 2, G - 1, G):
        stage(*near(g))


INPUTS = {"x": "x", "src": "src", "dst": "dst", "edge_attr": "edge_attr_32", "edge_weight": "edge_weight",
          "w_in": "L0_gnn_w_in", "b_in": "L0_gnn_b_in", "w_f1": "L0_gnn_w_f1", "b_f1": "L0_gnn_b_f1",
          "w_f2": "L0_gnn_w_f2", "b_f2": "L0_gnn_b_f2", "w_o1": "L0_gnn_w_o1", "b_o1": "L0_gnn_b_o1",
          "w_o2": "L0_gnn_w_o2", "b_o2": "L0_gnn_b_o2", "W": "L1_gnn_W", "b": "L1_gnn_b",
          "gamma": "L1_gnn_gamma", "beta": "L1_gnn_beta"}


class Memory:

    def __init__(self, nc, ctx):
        def sb(name, shape, dt=F32):
            return ctx.enter_context(nc.sbuf_tensor(name, shape, dt))

        self.h_tab = nc.dram_tensor("h_tab", [NT, F], F32)
        self.h_parts = nc.dram_tensor("h_parts", [NT, 3 * F], BF16)
        self.y_tab = nc.dram_tensor("y_tab", [NT, D], F32)
        self.agg_tab = [nc.dram_tensor(f"agg_tab{k}", [NT, F], F32) for k in range(K)]
        self.out_tab = [nc.dram_tensor(f"out_tab{k}", [NT, D], F32) for k in range(K)]
        self.src_hl = nc.dram_tensor("src_hl", [GC * P, 2, GE], BF16)
        self.dst_hl = nc.dram_tensor("dst_hl", [GC * P, 2, GE], BF16)
        self.deg_tab = nc.dram_tensor("deg_tab", [2, NT], F32)
        self.dinv_tab = nc.dram_tensor("dinv_tab", [N], F32)

        self.xs = sb("xs", [NP, NC, D])
        self.arena = sb("arena", [P, NT])
        self.srcF = sb("srcF", [P, GPAD * J])
        self.dstF = sb("dstF", [P, GPAD * J])
        self.srcT = sb("srcT", [P, GPAD * J])
        self.ident = sb("ident", [P, P])
        self.below = sb("below", [P, P])
        self.iota_w = sb("iota_w", [P, P])
        self.trash = sb("trash", [P, 1])
        self.split = sb("split", [2, P], BF16)
        self.ones = sb("ones", [1, P])
        self.half = sb("half", [P, 1])
        self.base_bc = sb("base_bc", [P, GC * P])
        self.base_i = sb("base_i", [1, GC * P], I32)
        self.winid = sb("winid", [P, GC * P])
        self.flag_i = sb("flag_i", [1, 1], I32)
        self.zeros = sb("zeros", [P, ZERO_COLS])
        self.w_in_s = sb("w_in_s", [D, F])
        self.w1_s = sb("w1_s", [P, 2, P])
        self.w2_s = sb("w2_s", [P, P])
        self.wo1_s = sb("wo1_s", [F, D])
        self.wo2_s = sb("wo2_s", [D, D])
        self.W_s = sb("W_s", [D, D])
        self.bin_s = sb("bin_s", [P, F])
        self.b1_s = sb("b1_s", [P, 1])
        self.b2_s = sb("b2_s", [3, J * F], BF16)
        self.ones3 = sb("ones3", [3, P], BF16)
        self.bo1_s = sb("bo1_s", [D, 1])
        self.bo2_s = sb("bo2_s", [1, B * D])
        self.gbb = sb("gbb", [D, 3])
        self.dinv = sb("dinv", [NP, NC])
        self.work = sb("work", [P, WORK])
        self.ps = ctx.enter_context(nc.psum_tensor("ps", [P, 8, 512], F32))
        self.xs_flat = self.xs.rearrange("p c d -> p (c d)")
        self.agg_added = [ctx.enter_context(nc.semaphore(f"agg_added{k}")) for k in range(K)]
        self.out_added = [ctx.enter_context(nc.semaphore(f"out_added{k}")) for k in range(K)]


def zero_table(eng, table, width, zeros, done):
    flat = table.rearrange("(p r) d -> p (r d)", p=P)
    per = NT * width // P // 3
    for t in range(3):
        n = per // ZERO_COLS
        eng.dma_start(flat[:, t * per:(t + 1) * per].rearrange("p (n c) -> p n c", n=n),
                      zeros[:, :].unsqueeze(1).to_broadcast([P, n, ZERO_COLS])).then_inc(done, 16)


def setup(nc, m, io):
    ps, work = m.ps, m.work
    ig = {"src": m.arena[:, 0:4096].bitcast(I32), "dst": m.arena[:, 4096:8192].bitcast(I32)}
    fg = {"src": m.arena[:, 8192:12288], "dst": work[:, 6000:10096]}
    given = {"src": io["src"], "dst": io["dst"]}
    cols = {"src": m.srcF, "dst": m.dstF}
    rows = {"src": m.src_hl, "dst": m.dst_hl}
    hi_i = work[:, 0:1024].bitcast(I32)
    lo_i = work[:, 1024:2048].bitcast(I32)
    hl = [work[:, 2048 + 1024 * s:3072 + 1024 * s].bitcast(BF16).rearrange("p (t e) -> p t e", t=2)
          for s in range(2)]
    xT = [work[:, 4096 + 512 * s:4096 + 512 * s + BW] for s in range(2)]
    hb = [work[0:NP, 5120 + 256 * s:5376 + 256 * s] for s in range(2)]
    xb = [work[0:NP, 10100 + 512 * s:10612 + 512 * s] for s in range(2)]
    b2_f, b2_rest, b2_row = (work[0:3, 11128 + F * t:11128 + F * t + F] for t in range(3))
    b2_high, b2_mid, b2_low = (work[0:3, 11320 + 32 * t:11352 + 32 * t].bitcast(BF16) for t in range(3))
    hp = [work[0:NP, 384 * s:384 * s + 384].bitcast(BF16).rearrange("p (t n f) -> p t n f", t=B, n=3) for s in range(2)]
    h_rest = work[0:NP, 1024:1024 + B * F]
    lim = work[:, 5632:5632 + 4 * GC]
    spans = work[0:1, 5700:5700 + P]
    flag_f = work[0:1, 5900:5901]
    psT = [ps[:, 0, 0:BW], ps[:, 1, 0:BW]]
    psH = [ps[0:NP, 2, 0:B * F], ps[0:NP, 3, 0:B * F]]
    psC = [ps[:, 4, :], ps[:, 5, :]]
    psM = ps[:, 6, :]
    psS = ps[:, 7, :]
    with ExitStack() as ctx:
        def sem(name):
            return ctx.enter_context(nc.semaphore(name))
        s_x, s_w, s_wdiag, s_idx = sem("x_in"), sem("weights_in"), sem("w1_in"), {"src": sem("src_in"), "dst": sem("dst_in")}
        s_pad, s_const, s_pool = sem("pad_set"), sem("consts_set"), sem("pool_consts")
        s_fg, s_cols, s_colsdone = sem("idx_float"), sem("cols_turned"), sem("cols_copied")
        s_hl, s_hlst = sem("hl_made"), [sem("hl_stored0"), sem("hl_stored1")]
        s_int = sem("hl_ints")
        s_lim, s_limT, s_bc = sem("limits"), sem("limits_turned"), sem("bases_out")
        s_sp, s_fl, s_trash = sem("span_row"), sem("flag_steps"), sem("trash_set")
        s_xT, s_xTc, s_h, s_hb = sem("x_turned"), sem("xT_copied"), sem("h_made"), sem("h_biased")
        s_hst, s_hpad = [sem("h_stored0"), sem("h_stored1")], sem("h_pad_stored")
        s_srcT, s_turn = sem("srcT_made"), sem("turn_order")
        s_b2, s_b2in = sem("b2_split"), sem("b2_in")
        s_split = sem("h_split")
        block = ctx.enter_context(nc.Block())
        s_xb = [sem("x_batch0"), sem("x_batch1")]
        x_rows = io["x"].rearrange("(p c) d -> p (c d)", p=NP)
        h_rows = m.h_tab[0:N, :].rearrange("(p c) d -> p (c d)", p=NP)
        NW = 13
        hp_rows = m.h_parts[0:N, :].rearrange("(p c) d -> p (c d)", p=NP)

        @block.sync
        def _(sp):
            for name in ("src", "dst"):
                a, t = given[name], ig[name]
                sp.wait_ge(s_pad, 1 if name == "src" else 2)
                full = G // P
                sp.dma_start(t.rearrange("p (c e) -> p c e", c=GC)[:, 0:full, :],
                             a[0:full * P * GE].rearrange("(c p e) -> p c e", p=P, e=GE)).then_inc(s_idx[name], 16)
                rest = G - 1 - full * P
                sp.dma_start(t[0:rest, full * GE:(full + 1) * GE],
                             a[full * P * GE:(G - 1) * GE].rearrange("(p e) -> p e", e=GE)).then_inc(s_idx[name], 16)
                sp.dma_start(t[rest:rest + 1, full * GE + SEEN:(full + 1) * GE],
                             a[(G - 1) * GE:E].rearrange("(p e) -> p e", p=1)).then_inc(s_idx[name], 16)
            sp.dma_start(m.xs_flat[:, :], io["x"].rearrange("(p c) d -> p (c d)", p=NP)).then_inc(s_x, 16)
            for n in range(2 * GC):
                name, c = ("src", "dst")[n // GC], n % GC
                sp.wait_ge(s_hl, n + 1)
                sp.dma_start(rows[name][c * P:(c + 1) * P, :, :], hl[n % 2]).then_inc(s_hlst[n % 2], 16)
            def store(q, s, turn):
                sp.wait_ge(s_split, 4 * q + 4)
                sp.dma_start(h_rows[:, bass.ds(q * (B * F), B * F)], hb[s]).then_inc(s_hst[s], 16)
                sp.dma_start(hp_rows[:, bass.ds(q * (B * 3 * F), B * 3 * F)],
                             hp[s].rearrange("p t n f -> p (t n f)")).then_inc(s_hst[s], 16)
            def load_x(q, s):
                sp.dma_start(xb[s], x_rows[:, bass.ds(q * (B * D), B * D)]).then_inc(s_xb[s], 16)

            def store_and_load(q, s, turn):
                store(q, s, turn)
                load_x(q + 2, s)
            load_x(0, 0)
            load_x(1, 1)
            over(sp, NB - 2, store_and_load)
            store(NB - 2, 1, NB // 2 - 1)
            store(NB - 1, 0, NB // 2)
            sp.wait_ge(s_hst[0], 32 * (NB // 2 + 1) + 32)
            sp.wait_ge(s_hst[1], 32 * (NB // 2) + 32)
            sp.wait_ge(s_x, 16)
            sp.wait_ge(s_hlst[0], 16 * GC)
            sp.wait_ge(s_hlst[1], 16 * GC)

        @block.scalar
        def _(act):
            act.wait_ge(s_const, 1)
            for t in range(4):
                act.dma_start(m.w1_s[R * t:R * t + R, t // 2, F * (t % 2):F * (t % 2) + F], io["w_f1"]).then_inc(s_wdiag, 16)
            act.dma_start(m.w_in_s[:, :], io["w_in"]).then_inc(s_w, 16)
            for t in range(2):
                act.dma_start(m.w2_s[F * t:F * t + F, F * t:F * t + F], io["w_f2"]).then_inc(s_w, 16)
                act.dma_start(m.b1_s[F * t:F * t + F, :], io["b_f1"].rearrange("(p o) -> p o", o=1)).then_inc(s_w, 16)
            act.dma_start(m.wo1_s[:, :], io["w_o1"]).then_inc(s_w, 16)
            act.dma_start(m.wo2_s[:, :], io["w_o2"]).then_inc(s_w, 16)
            act.dma_start(m.W_s[:, :], io["W"]).then_inc(s_w, 16)
            act.dma_start(m.bin_s[:, :], io["b_in"].rearrange("(o d) -> o d", o=1).to_broadcast([P, F])).then_inc(s_w, 16)
            act.dma_start(b2_f, io["b_f2"].rearrange("(o d) -> o d", o=1).to_broadcast([3, F])).then_inc(s_b2in, 16)
            act.dma_start(m.bo1_s[:, :], io["b_o1"].rearrange("(p o) -> p o", o=1)).then_inc(s_w, 16)
            act.dma_start(m.bo2_s[:, :].rearrange("o (j d) -> o j d", j=B),
                          io["b_o2"].rearrange("(o i d) -> o i d", o=1, i=1).to_broadcast([1, B, D])).then_inc(s_w, 16)
            for t, v in enumerate((io["b"], io["gamma"], io["beta"])):
                act.dma_start(m.gbb[:, t:t + 1], v.rearrange("(p o) -> p o", o=1)).then_inc(s_w, 16)
            act.dma_start(m.h_tab[N:NT, :].rearrange("(p r) d -> p (r d)", r=2), m.zeros[0:(NT - N) // 2, 0:2 * F]).then_inc(s_hpad, 16)
            act.dma_start(m.h_parts[N:NT, :].rearrange("(p r) d -> p (r d)", r=2),
                          m.zeros[0:(NT - N) // 2, 0:3 * F].bitcast(BF16)).then_inc(s_hpad, 16)
            act.dma_start(m.y_tab[N:NT, :].rearrange("(p r) d -> p (r d)", r=2), m.zeros[0:(NT - N) // 2, 0:2 * D]).then_inc(s_hpad, 16)
            act.sem_inc(s_xTc, 2)
            def copy(q, s, turn):
                act.wait_ge(s_xT, ready(q, 0))
                act.wait_ge(s_h, free(q))
                nc.scalar.copy(xT[s], psT[s]).then_inc(s_xTc, 1)
            over(act, NB, copy)
            act.wait_ge(s_hpad, 48)
            act.wait_ge(s_w, 16 * (NW + 1))
            act.wait_ge(s_wdiag, 64)

        @block.gpsimd
        def _(pool):
            nc.gpsimd.memset(m.ident[:, :], 0.0).then_inc(s_pool, 1)
            nc.gpsimd.memset(m.below[:, :], 1.0).then_inc(s_pool, 1)
            pool.wait_ge(s_pool, 2)
            nc.gpsimd.affine_select(out=m.ident[:, :], in_=m.ident[:, :], compare_op=ALU.not_equal, fill=1.0,
                                    base=0, pattern=[[-1, P]], channel_multiplier=1).then_inc(s_pool, 1)
            nc.gpsimd.affine_select(out=m.below[:, :], in_=m.below[:, :], compare_op=ALU.is_ge, fill=0.0,
                                    base=0, pattern=[[-1, P]], channel_multiplier=1).then_inc(s_pool, 1)
            nc.gpsimd.iota(m.iota_w[:, :], [[1, P]], base=0, channel_multiplier=0,
                           allow_small_or_imprecise_dtypes=True).then_inc(s_pool, 1)
            nc.gpsimd.iota(m.trash[:, :], [[0, 1]], base=TRASH, channel_multiplier=1,
                           allow_small_or_imprecise_dtypes=True).then_inc(s_pool, 1)
            pool.wait_ge(s_const, 1)
            for k in range(K):
                zero_table(pool, m.agg_tab[k], F, m.zeros, m.agg_added[k])
            for k in range(K):
                pool.wait_ge(m.agg_added[k], ZEROED)

        @block.tensor
        def _(pe):
            pe.wait_ge(s_pool, 4)
            pe.wait_ge(s_const, 4)
            n = 0
            for a, name in enumerate(("src", "dst")):
                pe.wait_ge(s_fg, a + 1)
                v = fg[name].rearrange("p (c e j) -> p c j e", c=GC, j=J)
                for c in range(GC):
                    ng = P if (c + 1) * P <= GPAD else GPAD - c * P
                    for jh in range(2):
                        if n >= 2:
                            pe.wait_ge(s_colsdone, n - 1)
                        for j in range(4):
                            t = pe.transpose(psC[n % 2][:, P * j:P * j + ng], v[0:ng, c, 4 * jh + j, :],
                                             m.ident[0:ng, 0:ng])
                        t.then_inc(s_cols, 1)
                        n += 1
            pe.wait_ge(s_lim, 4)
            for c in range(GC):
                t = pe.matmul(psM[:, c * P:(c + 1) * P], lim[:, c:c + 1].to_broadcast([P, P]), m.ident[:, :],
                              start=True, stop=True)
            t.then_inc(s_limT, 1)
            pe.transpose(psS[0:1, 0:P], lim[:, 3 * GC:3 * GC + 1], m.ident[:, :]).then_inc(s_limT, 1)
            pe.wait_ge(s_w, 16 * (NW + 1))
            pe.sem_inc(s_h, 2)
            def turn(q, s, turn_):
                pe.wait_ge(s_xb[s], 16 * turn_ + 16)
                pe.wait_ge(s_xTc, free(q))
                for t in range(B):
                    tr = pe.transpose(psT[s][:, NP * t:NP * t + NP], xb[s][:, D * t:D * t + D],
                                      m.ident[0:NP, 0:NP])
                tr.then_inc(s_xT, 1)
                pe.wait_ge(s_xTc, ready(q, 2))
                pe.wait_ge(s_hb, free(q))
                for t in range(B):
                    mm = pe.matmul(psH[s][:, F * t:F * t + F], xT[s][:, NP * t:NP * t + NP], m.w_in_s[:, :],
                                   start=True, stop=True)
                mm.then_inc(s_h, 1)
            over(pe, NB, turn)

        @block.vector
        def _(dve):
            nc.vector.memset(m.w1_s[:, :, :], 0.0)
            nc.vector.memset(m.w2_s[:, :], 0.0)
            nc.vector.memset(m.zeros[:, :], 0.0).then_inc(s_const, 1)
            nc.vector.memset(ig["src"][:, (GC - 1) * GE:GC * GE], PAD_NODE).then_inc(s_pad, 1)
            nc.vector.memset(ig["dst"][:, (GC - 1) * GE:GC * GE], PAD_NODE).then_inc(s_pad, 1)
            nc.vector.memset(m.half[:, :], 0.5)
            nc.vector.memset(m.ones3[:, :], 1.0)
            nc.vector.memset(m.ones[:, :], 1.0).then_inc(s_const, 1)
            nc.vector.memset(m.split[:, :], 1.0).then_inc(s_const, 1)
            dve.wait_ge(s_const, 3)
            nc.vector.memset(m.split[0:1, :], float(P)).then_inc(s_const, 1)
            for a, name in enumerate(("src", "dst")):
                dve.wait_ge(s_idx[name], 48)
                nc.vector.tensor_copy(fg[name], ig[name]).then_inc(s_fg, 1)
            dve.wait_ge(s_fg, 2)
            v = fg["dst"].rearrange("p (c e) -> p c e", c=GC)
            nc.vector.tensor_reduce(lim[:, 0:GC], v, AX.X, ALU.min).then_inc(s_lim, 1)
            nc.vector.tensor_reduce(lim[:, GC:2 * GC], v, AX.X, ALU.max).then_inc(s_lim, 1)
            dve.wait_ge(s_lim, 2)
            nc.vector.tensor_tensor(lim[:, 2 * GC:3 * GC], lim[:, GC:2 * GC], lim[:, 0:GC],
                                    ALU.subtract).then_inc(s_lim, 1)
            dve.wait_ge(s_lim, 3)
            nc.vector.tensor_reduce(lim[:, 3 * GC:3 * GC + 1], lim[:, 2 * GC:3 * GC], AX.X, ALU.max).then_inc(s_lim, 1)
            n = 0
            for name in ("src", "dst"):
                o = cols[name].rearrange("p (g j) -> p j g", j=J)
                for c in range(GC):
                    ng = P if (c + 1) * P <= GPAD else GPAD - c * P
                    for jh in range(2):
                        dve.wait_ge(s_cols, n + 1)
                        nc.vector.tensor_copy(o[:, 4 * jh:4 * jh + 4, c * P:c * P + ng],
                                              psC[n % 2].rearrange("p (j g) -> p j g", j=4)[:, :, 0:ng]).then_inc(s_colsdone, 1)
                        n += 1
            dve.wait_ge(s_pool, 6)
            dve.wait_ge(s_colsdone, n)
            nc.vector.tensor_scalar(m.srcT[:, :], m.srcF[:, :], m.trash[:, 0:1], None, ALU.subtract).then_inc(s_srcT, 1)
            for n in range(2 * GC):
                name, c = ("src", "dst")[n // GC], n % GC
                piece = ig[name][:, c * GE:(c + 1) * GE]
                if n >= 1:
                    dve.wait_ge(s_hl, n)
                nc.vector.tensor_scalar(hi_i, piece, 7, None, ALU.logical_shift_right).then_inc(s_int, 1)
                nc.vector.tensor_scalar(lo_i, piece, P - 1, None, ALU.bitwise_and).then_inc(s_int, 1)
                dve.wait_ge(s_int, 2 * n + 2)
                if n >= 2:
                    dve.wait_ge(s_hlst[n % 2], 16 * (n // 2))
                nc.vector.tensor_copy(hl[n % 2][:, 0, :], hi_i)
                nc.vector.tensor_copy(hl[n % 2][:, 1, :], lo_i).then_inc(s_hl, 1)
            dve.wait_ge(s_limT, 2)
            nc.vector.tensor_copy(m.base_bc[:, :], psM).then_inc(s_bc, 1)
            nc.vector.tensor_copy(m.base_i[:, :], psM[0:1, :]).then_inc(s_bc, 1)
            nc.vector.tensor_scalar(work[:, 5950:5951], m.trash[:, 0:1], float(TRASH), None, ALU.subtract).then_inc(s_bc, 1)
            dve.wait_ge(s_bc, 3)
            nc.vector.tensor_scalar(m.winid[:, :], m.base_bc[:, :], work[:, 5950:5951], None, ALU.add).then_inc(s_bc, 1)
            nc.vector.tensor_reduce(flag_f, psS[0:1, 0:P], AX.X, ALU.max).then_inc(s_fl, 1)
            dve.wait_ge(s_fl, 1)
            nc.vector.tensor_scalar(m.flag_i[:, :], flag_f, float(P), None, ALU.is_lt).then_inc(s_fl, 1)
            dve.wait_ge(s_b2in, 16)
            nc.vector.tensor_copy(b2_high, b2_f).then_inc(s_b2, 1)
            dve.wait_ge(s_b2, 1)
            nc.vector.tensor_tensor(b2_rest, b2_f, b2_high, ALU.subtract).then_inc(s_b2, 1)
            nc.vector.tensor_scalar(b2_row, b2_high, m.ident[0:3, 0:1], None, ALU.mult).then_inc(s_b2, 1)
            dve.wait_ge(s_b2, 3)
            nc.vector.tensor_copy(b2_mid, b2_rest).then_inc(s_b2, 1)
            dve.wait_ge(s_b2, 4)
            nc.vector.tensor_tensor(b2_low, b2_rest, b2_mid, ALU.subtract).then_inc(s_b2, 1)
            nc.vector.scalar_tensor_tensor(b2_row, b2_mid, m.ident[0:3, 1:2], b2_row, ALU.mult, ALU.add).then_inc(s_b2, 1)
            dve.wait_ge(s_b2, 6)
            for j in range(J):
                nc.vector.scalar_tensor_tensor(m.b2_s[:, F * j:F * j + F], b2_low, m.ident[0:3, 2:3], b2_row,
                                               ALU.mult, ALU.add).then_inc(s_b2, 1)
            dve.sem_inc(s_hb, 2)
            dve.sem_inc(s_hst[0], 32)
            dve.sem_inc(s_hst[1], 32)
            dve.wait_ge(s_hl, 2 * GC)
            def bias(q, s, turn):
                dve.wait_ge(s_h, ready(q, 2))
                dve.wait_ge(s_hst[s], 32 * turn + 32)
                nc.vector.tensor_tensor(hb[s].rearrange("p (t f) -> p t f", t=B),
                                        psH[s].rearrange("p (t f) -> p t f", t=B),
                                        m.bin_s[0:NP, :].unsqueeze(1).to_broadcast([NP, B, F]), ALU.add).then_inc(s_hb, 1)
                dve.wait_ge(s_hb, ready(q, 2))
                h4, rest4 = (v.rearrange("p (t f) -> p t f", t=B) for v in (hb[s], h_rest))
                nc.vector.tensor_copy(hp[s][:, :, 0, :], h4).then_inc(s_split, 1)
                dve.wait_ge(s_split, 4 * q + 1)
                nc.vector.tensor_tensor(rest4, h4, hp[s][:, :, 0, :], ALU.subtract).then_inc(s_split, 1)
                dve.wait_ge(s_split, 4 * q + 2)
                nc.vector.tensor_copy(hp[s][:, :, 1, :], rest4).then_inc(s_split, 1)
                dve.wait_ge(s_split, 4 * q + 3)
                nc.vector.tensor_tensor(hp[s][:, :, 2, :], rest4, hp[s][:, :, 1, :], ALU.subtract).then_inc(s_split, 1)
            over(dve, NB, bias)


def filter_layer(nc, m, io):
    ps, work = m.ps, m.work

    def slots(at, width, n=2):
        return [work[:, at + width * s:at + width * s + width] for s in range(n)]

    attr = slots(0, J * R)
    weight = slots(512, J)
    srow = [v[0:2, :].bitcast(BF16) for v in slots(544, GE // 2)]
    drow = [v[0:2, :].bitcast(BF16) for v in slots(1568, GE // 2)]
    hwin = [v.bitcast(BF16) for v in slots(2640, 3 * F // 2)]
    attrT = work[:, 2832:3088]
    log1p = work[:, 3088:3600]
    relu = work[:, 3600:4112]
    hid = slots(4112, 512)
    pick = [v.bitcast(BF16) for v in slots(5136, J * P // 2)]
    same = [v.bitcast(BF16) for v in slots(7136, J * P // 2)]
    weighed = work[:, 8160:8672]
    msg = work[:, 8672:9184]
    parts = [v.bitcast(BF16) for v in slots(9184, 3 * J * F // 2)]
    summed = slots(10720, J * F)
    sidx = [v.bitcast(U32) for v in slots(11744, J)]
    earlier = slots(11760, J)
    first = work[:, 11776:11776 + J]
    count = slots(11784, 2)
    gidx = [v.bitcast(U32) for v in slots(11788, J)]
    grow = slots(5136, J * F)
    one_lo = work[:, 6160:6672].bitcast(BF16)
    one_hi = work[:, 6672:6672 + 396].bitcast(BF16)
    dst_i = work[:, 2592:2592 + J].bitcast(I32)
    lo_i = work[:, 2600:2600 + J].bitcast(I32)
    hi_i = work[:, 2608:2608 + J].bitcast(I32)
    lo_f = work[:, 2616:2616 + J]
    hi_f = work[:, 2624:2624 + J]
    NHI = NT // P
    deg_hl = work[0:NHI, 8160:8160 + P]
    degrow = m.arena[0:2, :]

    ps_attr = ps[:, 1, 0:2 * P]
    ps_deg = ps[0:2, 0, 0:P]
    ps_hid = ps[:, 1, :]
    ps_filt = ps[:, 2, :]
    ps_row = ps[:, 3, :]
    ps_sum = ps[:, 4, :]
    ps_src = ps[:, 5:7, :].rearrange("p a b -> p (a b)")
    ps_dst = ps[:, 7, :]

    with ExitStack() as ctx:
        def sem(name):
            return ctx.enter_context(nc.semaphore(name))
        edges_in = [sem("edges_loaded0"), sem("edges_loaded1")]
        window_in = [sem("window_loaded0"), sem("window_loaded1")]
        gathered = [sem("rows_gathered0"), sem("rows_gathered1")]
        attr_turned, attr_copied, hid_made, ln_made, hid_done = (
            sem("attr_turned"), sem("attr_copied"), sem("hid_made"), sem("ln_made"), sem("hid_done"))
        act_steps, window_turn = sem("act_steps"), sem("window_turn")
        src_out, dst_out, same_done, pick_done = (
            sem("src_broadcast"), sem("dst_broadcast"), sem("same_done"), sem("pick_done"))
        filt_made, row_picked, weighed_done, msg_done = (
            sem("filter_made"), sem("rows_picked"), sem("weighed_done"), sem("msg_done"))
        high_done, rest_done, mid_done, low_done = sem("high_done"), sem("rest_done"), sem("mid_done"), sem("low_done")
        sum_made, sum_copied, first_done, idx_done = (
            sem("sum_made"), sem("sum_copied"), sem("first_done"), sem("idx_done"))
        deg_turned, deg_added, gidx_done, pool_turn = (
            sem("deg_turned"), sem("deg_added"), sem("gidx_done"), sem("pool_turn"))
        digits, onehots, deg_counted, deg_stored = (
            sem("dst_digits"), sem("onehots_done"), sem("deg_counted"), sem("deg_stored"))
        deg_final = sem("deg_final")
        block = ctx.enter_context(nc.Block())

        def load_edges(sp, g, s, turn, windows, last=False):
            at = E - GE if last else g * GE
            sp.dma_start(attr[s], io["edge_attr"][bass.ds(at, GE), :].rearrange("(p j) r -> p (j r)", p=P)).then_inc(edges_in[s], 16)
            sp.dma_start(srow[s], m.src_hl[bass.ds(g, 1), :, :].rearrange("o t e -> (o t) e")).then_inc(edges_in[s], 16)
            if windows:
                sp.dma_start(drow[s], m.dst_hl[bass.ds(g, 1), :, :].rearrange("o t e -> (o t) e")).then_inc(edges_in[s], 16)

        def load_window(sp, g, s, turn, windows, last=False):
            at = E - GE if last else g * GE
            sp.dma_start(weight[s], io["edge_weight"][bass.ds(at, GE)].rearrange("(p j) -> p j", p=P)).then_inc(window_in[s], 16)
            if windows:
                base = sp.value_load(m.base_i[0:1, bass.ds(g, 1)], min_val=0, max_val=N)
                sp.dma_start(hwin[s], m.h_parts[bass.ds(base, P), :]).then_inc(window_in[s], 16)

        def sync_way(sp, windows):
            def slot_read(before):
                if windows:
                    sp.wait_ge(dst_out, 2 * before)
                else:
                    sp.wait_ge(src_out, before)

            load_edges(sp, 0, 0, 0, windows)
            load_edges(sp, 1, 1, 0, windows)
            load_window(sp, 0, 0, 0, windows)
            with sp.Fori(0, (G - 3) // 2) as i:
                for s in range(2):
                    k, before = 2 * i + s + 2, 2 * i + s + 1
                    slot_read(before)
                    load_edges(sp, k, s, i + 1, windows)
                    sp.wait_ge(msg_done, before)
                    sp.sem_inc(window_turn, 1)
                    load_window(sp, before, 1 - s, i + s, windows)
            slot_read(G - 2)
            load_edges(sp, G - 1, 0, 0, windows, last=True)
            sp.wait_ge(msg_done, G - 2)
            load_window(sp, G - 2, 1, 0, windows)
            sp.wait_ge(msg_done, G - 1)
            load_window(sp, G - 1, 0, 0, windows, last=True)

        @block.sync
        def _(sp):
            flag = sp.value_load(m.flag_i[0:1, 0:1], min_val=0, max_val=1)
            with sp.If(flag == 1):
                sync_way(sp, True)
                sp.wait_ge(deg_final, 1)
                sp.dma_start(m.deg_tab[:, :], degrow).then_inc(deg_stored, 16)
            with sp.Else():
                sync_way(sp, False)
                sp.wait_ge(deg_final, 1)
                sp.dma_start(m.deg_tab[0, :].rearrange("(h l) -> h l", l=P), deg_hl).then_inc(deg_stored, 16)
                sp.dma_start(m.deg_tab[1, :].rearrange("(h l) -> h l", l=P), m.zeros[0:NHI, 0:P]).then_inc(deg_stored, 16)
                sp.wait_ge(deg_stored, 32)
            sp.wait_ge(deg_stored, 16)

        def pe_hidden(pe, g, s, turn, windows):
            pe.wait_ge(edges_in[s], 16 * (3 if windows else 2) * (turn + 1))
            pe.wait_ge(ln_made, free(g))
            for q in range(2):
                t = pe.transpose(ps_attr[:, P * q:P * q + P], attr[s][:, P * q:P * q + P], m.ident[:, :])
            t.then_inc(attr_turned, 1)
            if windows:
                pe_dst(pe, g, s, 0)
            pe.wait_ge(attr_copied, ready(g, 1))
            for q in range(4):
                mm = pe.matmul(ps_hid[:, P * q:P * q + P], m.w1_s[:, q % 2, :], attrT[:, P * (q // 2):P * (q // 2) + P],
                               start=True, stop=True)
            mm.then_inc(hid_made, 1)

        def pe_src(pe, g, s):
            pe.wait_ge(same_done, free(g))
            for q in range(2):
                mm = pe.matmul(ps_src[:, 512 * q:512 * q + 512], m.split[:, :], srow[s][:, 512 * q:512 * q + 512],
                               start=True, stop=True)
            mm.then_inc(src_out, 1)

        def pe_dst(pe, g, s, q):
            pe.wait_ge(pick_done, 2 * g + q + 1)
            pe.matmul(ps_dst, m.split[:, :], drow[s][:, 512 * q:512 * q + 512], start=True, stop=True).then_inc(dst_out, 1)

        def pe_filter(pe, g, s):
            pe.wait_ge(hid_done, ready(g, 1))
            pe.wait_ge(weighed_done, free(g))
            pe.matmul(ps_filt, m.ones3[:, :], m.b2_s[:, :], start=True, stop=False, skip_group_check=True)
            for q in range(J // 2):
                mm = pe.matmul(ps_filt[:, P * q:P * q + P], hid[s][:, P * q:P * q + P], m.w2_s[:, :],
                               start=False, stop=(q == J // 2 - 1), skip_group_check=True)
            mm.then_inc(filt_made, 1)

        def pe_rows(pe, g, s, turn, windows):
            pe.wait_ge(window_in[s], 16 * (2 if windows else 1) * (turn + 1))
            if windows:
                pe.wait_ge(pick_done, 2 * g + 3)
                pe.wait_ge(msg_done, free(g))
                for j in range(J):
                    for n in range(3):
                        mm = pe.matmul(ps_row[:, F * j:F * j + F], pick[s][:, P * j:P * j + P], hwin[s][:, F * n:F * n + F],
                                       start=(n == 0), stop=(n == 2))
                mm.then_inc(row_picked, 1)
            else:
                pe.wait_ge(onehots, ready(g, 0))
                for j in range(J):
                    mm = pe.matmul(ps_dst[0:NHI, 0:P], one_hi.rearrange("p (j h) -> p j h", j=J)[:, j, :],
                                   one_lo[:, P * j:P * j + P], start=False, stop=False, skip_group_check=True)
                mm.then_inc(deg_counted, 1)

        def pe_degrees(pe, g, s):
            pe.wait_ge(deg_added, free(g))
            pe.matmul(ps_deg, count[s], m.ident[:, :], start=True, stop=True).then_inc(deg_turned, 1)

        def pe_sums(pe, g, s):
            pe.wait_ge(same_done, ready(g, 1))
            pe.wait_ge(low_done, ready(g, 1))
            pe.wait_ge(sum_copied, free(g))
            for j in range(J):
                for n in range(3):
                    at = J * F * n + F * j
                    mm = pe.matmul(ps_sum[:, F * j:F * j + F], same[s][:, P * j:P * j + P], parts[s][:, at:at + F],
                                   start=(n == 0), stop=(n == 2))
            mm.then_inc(sum_made, 1)

        def tensor_way(pe, windows):
            def stage(before, here, after):
                if after:
                    pe_hidden(pe, *after, windows)
                if here:
                    pe_rows(pe, *here, windows)
                    pe_filter(pe, *here[:2])
                if after:
                    pe_src(pe, *after[:2])
                if here and windows:
                    pe_degrees(pe, *here[:2])
                if before:
                    pe_sums(pe, *before[:2])
                if after and windows:
                    pe_dst(pe, *after[:2], 1)
            staged(pe, stage)

        @block.tensor
        def _(pe):
            pe.sem_inc(sum_made, 2)
            pe.sem_inc(row_picked, 2)
            pe.sem_inc(filt_made, 2)
            pe.sem_inc(hid_made, 1)
            pe.sem_inc(deg_counted, 1)
            flag = pe.value_load(m.flag_i[0:1, 0:1], min_val=0, max_val=1)
            with pe.If(flag == 1):
                tensor_way(pe, True)
            with pe.Else():
                pe.matmul(ps_dst[0:NHI, 0:P], m.zeros[0:1, 0:NHI], m.zeros[0:1, 0:P], start=True, stop=False,
                          skip_group_check=True)
                tensor_way(pe, False)
            pe.wait_ge(attr_turned, G)

        def act_stage(act, before, here, after):
            if after:
                g = after[0]
                act.wait_ge(attr_turned, ready(g, 0))
                act.wait_ge(hid_made, free(g))
                nc.scalar.copy(attrT, ps_attr).then_inc(attr_copied, 1)
            if before:
                g, s, _ = before
                act.wait_ge(msg_done, ready(g, 1))
                act.wait_ge(sum_made, free(g))
                nc.scalar.copy(parts[s][:, 0:J * F], msg).then_inc(high_done, 1)
            if after:
                g = after[0]
                act.wait_ge(hid_made, ready(g, 1))
                act.wait_ge(hid_done, free(g))
                nc.scalar.activation(log1p, ps_hid, ACT.Abs, bias=m.b1_s[:, 0:1]).then_inc(act_steps, 1)
            if before:
                g, s, _ = before
                act.wait_ge(rest_done, ready(g, 0))
                nc.scalar.copy(parts[s][:, J * F:2 * J * F], msg).then_inc(mid_done, 1)
            if after:
                g = after[0]
                nc.scalar.activation(relu, ps_hid, ACT.Relu, bias=m.b1_s[:, 0:1])
                act.wait_ge(act_steps, 2 * g + 1)
                nc.scalar.activation(log1p, log1p, ACT.Exp, scale=-1.0).then_inc(act_steps, 1)
                act.wait_ge(act_steps, 2 * g + 2)
                nc.scalar.activation(log1p, log1p, ACT.Ln, scale=0.5, bias=m.half[:, 0:1]).then_inc(ln_made, 1)
            if before:
                g, s, _ = before
                act.wait_ge(sum_made, ready(g, 2))
                for k in range(K):
                    act.wait_ge(m.agg_added[k], 32 * g + ZEROED - 32)
                nc.scalar.copy(summed[s], ps_sum).then_inc(sum_copied, 1)

        @block.scalar
        def _(act):
            act.preload_act_table_set("natural_log_exp_and_others")
            act.sem_inc(attr_copied, 1)
            act.sem_inc(ln_made, 1)
            act.sem_inc(sum_copied, 1)

            staged(act, lambda before, here, after: act_stage(act, before, here, after))

        def dve_pick(dve, g, s, q):
            if q == 0:
                dve.wait_ge(row_picked, free(g))
                if not isinstance(g, int):
                    dve.wait_ge(deg_turned, g - 1)
            dve.wait_ge(dst_out, 2 * g + q + 1)
            half = P // 2
            nc.vector.tensor_scalar(pick[s].rearrange("w (j e) -> w e j", j=J)[:, half * q:half * q + half, :],
                                    ps_dst.rearrange("w (e j) -> w e j", j=J), m.winid[:, bass.ds(g, 1)], 0.0,
                                    ALU.is_equal, ALU.add, accum_out=count[s][:, q:q + 1]).then_inc(pick_done, 1)

        def dve_onehots(dve, g, s):
            nc.vector.tensor_copy(dst_i, m.dstF[:, bass.ds(g * J, J)]).then_inc(digits, 1)
            dve.wait_ge(digits, 5 * g + 1)
            nc.vector.tensor_scalar(hi_i, dst_i, 7, None, ALU.logical_shift_right).then_inc(digits, 1)
            nc.vector.tensor_scalar(lo_i, dst_i, P - 1, None, ALU.bitwise_and).then_inc(digits, 1)
            dve.wait_ge(digits, 5 * g + 3)
            nc.vector.tensor_copy(hi_f, hi_i).then_inc(digits, 1)
            nc.vector.tensor_copy(lo_f, lo_i).then_inc(digits, 1)
            dve.wait_ge(digits, 5 * g + 5)
            dve.wait_ge(deg_counted, free(g))
            for one, width, digit in ((one_lo, P, lo_f), (one_hi, NHI, hi_f)):
                last = nc.vector.tensor_tensor(one.rearrange("p (j h) -> p j h", j=J),
                                               m.iota_w[:, 0:width].unsqueeze(1).to_broadcast([P, J, width]),
                                               digit.unsqueeze(2).to_broadcast([P, J, width]), ALU.is_equal)
            last.then_inc(onehots, 1)

        def dve_gidx(dve, g, s):
            if not isinstance(g, int):
                dve.wait_ge(msg_done, g)
            nc.vector.tensor_copy(gidx[s], m.dstF[:, bass.ds(g * J, J)]).then_inc(gidx_done, 1)

        def dve_same(dve, g, s, turn, tiles):
            if 0 in tiles:
                dve.wait_ge(src_out, ready(g, 0))
                dve.wait_ge(sum_made, free(g))
            for j in tiles:
                mm = nc.vector.scalar_tensor_tensor(same[s][:, P * j:P * j + P], ps_src.rearrange("p (e j) -> p j e", j=J)[:, j, :],
                                                    m.srcF[:, bass.ds(g * J + j, 1)], m.below[:, :], ALU.is_equal, ALU.mult,
                                                    accum_out=earlier[s][:, j:j + 1])
            if J - 1 in tiles:
                mm.then_inc(same_done, 1)

        def dve_sidx(dve, g, s):
            dve.wait_ge(same_done, ready(g, 1))
            nc.vector.scalar_tensor_tensor(first, earlier[s], 1.0, m.srcT[:, bass.ds(g * J, J)], ALU.is_equal,
                                           ALU.mult).then_inc(first_done, 1)
            dve.wait_ge(first_done, ready(g, 0))
            for k in range(K):
                dve.wait_ge(m.agg_added[k], 32 * g + ZEROED - 32)
            nc.vector.tensor_scalar(sidx[s], first, m.trash[:, 0:1], None, ALU.add).then_inc(idx_done, 1)

        def dve_hidden(dve, g, s):
            dve.wait_ge(ln_made, ready(g, 1))
            dve.wait_ge(filt_made, free(g))
            nc.vector.tensor_tensor(hid[s], relu, log1p, ALU.add).then_inc(hid_done, 1)

        def dve_message(dve, g, s, turn, windows):
            dve.wait_ge(filt_made, ready(g, 2))
            nc.vector.tensor_tensor(weighed.rearrange("p (j f) -> p j f", j=J), ps_filt.rearrange("p (j f) -> p j f", j=J),
                                    weight[s].unsqueeze(2).to_broadcast([P, J, F]), ALU.mult).then_inc(weighed_done, 1)
            dve.wait_ge(weighed_done, ready(g, 1))
            if windows:
                dve.wait_ge(row_picked, ready(g, 2))
                rows = ps_row
            else:
                dve.wait_ge(gathered[s], 128 * turn + 128)
                rows = grow[s]
            dve.wait_ge(low_done, free(g))
            nc.vector.tensor_tensor(msg, rows, weighed, ALU.mult).then_inc(msg_done, 1)

        def dve_rest(dve, g, s):
            dve.wait_ge(high_done, ready(g, 0))
            nc.vector.tensor_tensor(msg, msg, parts[s][:, 0:J * F], ALU.subtract).then_inc(rest_done, 1)

        def dve_low(dve, g, s):
            dve.wait_ge(mid_done, ready(g, 0))
            nc.vector.tensor_tensor(parts[s][:, 2 * J * F:], msg, parts[s][:, J * F:2 * J * F], ALU.subtract).then_inc(low_done, 1)

        def dve_degrees(dve, g, windows):
            if windows:
                base = dve.value_load(m.base_i[0:1, bass.ds(g, 1)], min_val=0, max_val=N)
                dve.wait_ge(deg_turned, ready(g, 0))
                here = degrow[:, bass.ds(base, P)]
                nc.vector.tensor_tensor(here, here, ps_deg, ALU.add).then_inc(deg_added, 1)
                dve.wait_ge(deg_added, ready(g, 1))

        def vector_way(dve, windows):
            def stage(before, here, after):
                if before:
                    dve_message(dve, *before, windows)
                if here:
                    dve_same(dve, *here, range(0, J // 2))
                if before:
                    dve_rest(dve, *before[:2])
                if here:
                    dve_same(dve, *here, range(J // 2, J))
                if before:
                    dve_degrees(dve, before[0], windows)
                    dve_low(dve, *before[:2])
                    dve_sidx(dve, *before[:2])
                if after:
                    if windows:
                        dve_pick(dve, *after[:2], 0)
                    else:
                        dve_gidx(dve, *after[:2])
                    dve_hidden(dve, *after[:2])
                    if windows:
                        dve_pick(dve, *after[:2], 1)
                    else:
                        dve_onehots(dve, *after[:2])
            staged(dve, stage)

        @block.vector
        def _(dve):
            dve.sem_inc(hid_done, 1)
            dve.sem_inc(same_done, 1)
            dve.sem_inc(pick_done, 1)
            dve.sem_inc(weighed_done, 1)
            dve.sem_inc(msg_done, 1)
            dve.sem_inc(low_done, 1)
            nc.vector.memset(degrow, 0.0).then_inc(deg_added, 1)
            dve.wait_ge(deg_added, 1)
            flag = dve.value_load(m.flag_i[0:1, 0:1], min_val=0, max_val=1)
            with dve.If(flag == 1):
                vector_way(dve, True)
                dve.sem_inc(deg_final, 1)
            with dve.Else():
                vector_way(dve, False)
                dve.wait_ge(deg_counted, ready(G - 1, 1))
                dve.wait_ge(msg_done, ready(G - 1, 1))
                nc.vector.tensor_copy(deg_hl, ps_dst[0:NHI, 0:P]).then_inc(deg_final, 1)
            dve.wait_ge(deg_final, 1)

        def gather(pool, g, s, turn):
            pool.wait_ge(gidx_done, ready(g, 0))
            if not isinstance(g, int):
                pool.wait_ge(msg_done, g)
            pool.sem_inc(pool_turn, 1)
            for j in range(J):
                nc.gpsimd.indirect_dma_start(
                    out=grow[s][:, F * j:F * j + F], out_offset=None, in_=m.h_tab[:, :],
                    in_offset=bass.IndirectOffsetOnAxis(ap=gidx[s][:, j:j + 1], axis=0)).then_inc(gathered[s], 16)

        def scatter(pool, g, s, turn):
            pool.wait_ge(idx_done, ready(g, 0))
            pool.wait_ge(sum_copied, ready(g, 1))
            for j in range(J):
                k = j % K
                pool.wait_ge(m.agg_added[k], 32 * g + 16 * (j // K) + ZEROED)
                pool.sem_inc(pool_turn, 1)
                nc.gpsimd.indirect_dma_start(
                    out=m.agg_tab[k][:, :], out_offset=bass.IndirectOffsetOnAxis(ap=sidx[s][:, j:j + 1], axis=0),
                    in_=summed[s][:, F * j:F * j + F], in_offset=None,
                    compute_op=ALU.add).then_inc(m.agg_added[k], 16)

        @block.gpsimd
        def _(pool):
            flag = pool.value_load(m.flag_i[0:1, 0:1], min_val=0, max_val=1)
            with pool.If(flag == 1):
                over(pool, G, lambda g, s, turn: scatter(pool, g, s, turn))
            with pool.Else():
                def step(g, s, turn):
                    gather(pool, g + 1, 1 - s, turn + s)
                    scatter(pool, g, s, turn)
                pipelined(pool, G, lambda g, s, t: gather(pool, g, s, t), step, lambda g, s, t: scatter(pool, g, s, t))
            for k in range(K):
                pool.wait_ge(m.agg_added[k], 32 * G + ZEROED)


def layer_norm_stats(nc, dve, m, work_at, steps, waited, base, q, s, mv):
    dve.sem_inc(waited, 1)
    stats = m.work[0:NP, work_at:work_at + 6 * B].rearrange("p (t s) -> p t s", t=B)
    pair = m.work[0:NP, work_at + 6 * B:work_at + 8 * B].rearrange("p (t s) -> p t s", t=B)
    for t in range(B):
        last = nc.vector.bn_stats(stats[:, t, :], m.xs_flat[:, bass.ds(q * (B * D) + t * D, D)])
    last.then_inc(steps, 1)
    dve.wait_ge(steps, base + 1)
    dve.sem_inc(waited, 1)
    for t in range(B):
        last = nc.vector.bn_aggr(pair[:, t, :], stats[:, t, :])
    last.then_inc(steps, 1)
    dve.wait_ge(steps, base + 2)
    nc.vector.tensor_copy(mv[:, bass.ds(q * (2 * B), 2 * B)], pair.rearrange("p t s -> p (t s)")).then_inc(steps, 1)


def node_update(nc, m, io):
    ps, work = m.ps, m.work
    tabs = [work[0:NP, 1024 * s:1024 * s + K * B * F] for s in range(2)]
    agg = [work[0:NP, 2048 + 256 * s:2304 + 256 * s] for s in range(2)]
    aggT = [work[0:F, 2560 + 512 * s:2560 + 512 * s + BW] for s in range(2)]
    log1p = work[:, 3584:3584 + BW]
    relu = work[:, 4096:4096 + BW]
    hid = [work[:, 4608 + 512 * s:4608 + 512 * s + BW] for s in range(2)]
    LN_AT = 5632
    mv = work[0:NP, 5700:5700 + 2 * NC]
    rstd = work[0:NP, 5900:5900 + NC]
    var = work[0:NP, 6000:6000 + NC]
    xT = [work[:, 6144 + 512 * s:6144 + 512 * s + BW] for s in range(2)]
    yb = [work[0:NP, 7168 + 512 * s:7680 + 512 * s] for s in range(2)]
    deg2 = work[0:NP, 9300:9300 + NC]
    xn = [work[0:NP, 8192 + 512 * s:8704 + 512 * s] for s in range(2)]
    ps_a = [ps[0:F, s, 0:BW] for s in range(2)]
    ps_h = [ps[:, 2 + s, 0:BW] for s in range(2)]
    ps_o = [ps[0:NP, 4 + s, :] for s in range(2)]
    ps_xT = [ps[:, s, 0:BW] for s in range(2)]
    ps_y = [ps[0:NP, 2 + s, :] for s in range(2)]
    ps_yT = [ps[:, 4 + s, 0:BW] for s in range(2)]
    rows = m.arena[:, 0:N].rearrange("f (p c) -> f c p", c=NC)

    with ExitStack() as ctx:
        def sem(name):
            return ctx.enter_context(nc.semaphore(name))
        deg_in, dinv_steps, dinv_act, dinv_stored = sem("deg_in"), sem("dinv_steps"), sem("dinv_act"), sem("dinv_stored")
        tabs_in = [sem("tables_in0"), sem("tables_in1")]
        y_stored = [sem("y_stored0"), sem("y_stored1")]
        agg_sum, agg_turned, agg_copied = sem("agg_summed"), sem("agg_turned"), sem("agg_copied")
        hid_made, act_steps, ln_made, hid_done = sem("hidden_made"), sem("act_order"), sem("hidden_ln"), sem("hidden_done")
        waited = sem("ln_waited")
        out_made, res_done, steps = sem("out_made"), sem("residual_done"), sem("ln_steps")
        var_done, std_done, rstd_done = sem("var_done"), sem("std_done"), sem("rstd_done")
        x_done, x_turned, xT_copied = sem("x_normed"), sem("x_turned"), sem("xT_copied")
        x_kept, x_seen = sem("x_kept"), sem("x_seen")
        y_made, y_scaled, y_turned, yT_copied = sem("y_made"), sem("y_scaled"), sem("y_turned"), sem("yT_copied")
        block = ctx.enter_context(nc.Block())

        @block.sync
        def _(sp):
            sp.dma_start(m.dinv[:, :], m.deg_tab[0, 0:N].rearrange("(p c) -> p c", p=NP)).then_inc(deg_in, 16)
            sp.dma_start(deg2, m.deg_tab[1, 0:N].rearrange("(p c) -> p c", p=NP)).then_inc(deg_in, 16)

            def load(q, s, turn):
                sp.wait_ge(agg_sum, free(q))
                for k in range(K):
                    sp.dma_start(tabs[s][:, B * F * k:B * F * k + B * F],
                                 m.agg_tab[k][0:N, :].rearrange("(p c) d -> p (c d)", p=NP)[:, bass.ds(q * (B * F), B * F)]
                                 ).then_inc(tabs_in[s], 16)
            over(sp, NB, load)
            sp.wait_ge(dinv_steps, 2)
            sp.dma_start(m.dinv_tab.rearrange("(p c) -> p c", p=NP), m.dinv[:, :]).then_inc(dinv_stored, 16)

            def store(q, s, turn):
                sp.wait_ge(y_scaled, ready(q, 1))
                sp.dma_start(m.y_tab[0:N, :].rearrange("(p c) d -> p (c d)", p=NP)[:, bass.ds(q * (B * D), B * D)],
                             yb[s]).then_inc(y_stored[s], 16)
            over(sp, NB, store)
            sp.wait_ge(y_stored[0], 16 * (NB // 2 + 2))
            sp.wait_ge(y_stored[1], 16 * (NB // 2 + 1))
            sp.wait_ge(dinv_stored, 16)

        @block.tensor
        def _(pe):
            pe.sem_inc(agg_turned, 2)
            pe.sem_inc(hid_made, 2)
            pe.sem_inc(out_made, 2)

            def turn_agg(q, s):
                pe.wait_ge(agg_sum, ready(q, 2))
                pe.wait_ge(agg_copied, free(q))
                for t in range(B):
                    tr = pe.matmul(ps_a[s][:, NP * t:NP * t + NP], agg[s][:, F * t:F * t + F], m.ident[0:NP, 0:NP],
                                   start=True, stop=True)
                tr.then_inc(agg_turned, 1)

            def hidden(q, s):
                pe.wait_ge(agg_copied, ready(q, 2))
                pe.wait_ge(ln_made, free(q))
                pe.matmul(ps_h[s], m.wo1_s[:, :], aggT[s], start=True, stop=True).then_inc(hid_made, 1)

            def output(q, s):
                pe.wait_ge(hid_done, ready(q, 1))
                pe.wait_ge(res_done, free(q))
                pe.matmul(ps_o[s], m.ones[:, 0:NP], m.bo2_s[:, :], start=True, stop=False, skip_group_check=True)
                for t in range(B):
                    mm = pe.matmul(ps_o[s][:, D * t:D * t + D], hid[s][:, NP * t:NP * t + NP], m.wo2_s[:, :],
                                   start=False, stop=(t == B - 1), skip_group_check=True)
                mm.then_inc(out_made, 1)

            def first(q, s, turn):
                turn_agg(q, s)
                hidden(q, s)

            def step(q, s, turn):
                turn_agg(q + 1, 1 - s)
                hidden(q + 1, 1 - s)
                output(q, s)
            pipelined(pe, NB, first, step, lambda q, s, turn: output(q, s))

            pe.sem_inc(x_turned, 2)
            pe.sem_inc(y_made, 2)
            pe.sem_inc(y_turned, 2)

            def turn_x(q, s):
                pe.wait_ge(x_done, ready(q, 0))
                pe.wait_ge(xT_copied, free(q))
                for t in range(B):
                    tr = pe.transpose(ps_xT[s][:, NP * t:NP * t + NP], xn[s][:, D * t:D * t + D],
                                      m.ident[0:NP, 0:NP])
                tr.then_inc(x_turned, 1)

            def times_w(q, s):
                pe.wait_ge(xT_copied, ready(q, 2))
                if not isinstance(q, int):
                    pe.wait_ge(y_scaled, q)
                for t in range(B):
                    mm = pe.matmul(ps_y[s][:, D * t:D * t + D], xT[s][:, NP * t:NP * t + NP], m.W_s[:, :],
                                   start=True, stop=True)
                mm.then_inc(y_made, 1)

            def turn_y(q, s):
                pe.wait_ge(y_scaled, ready(q, 1))
                pe.wait_ge(yT_copied, free(q))
                for t in range(B):
                    tr = pe.transpose(ps_yT[s][:, NP * t:NP * t + NP], yb[s][:, D * t:D * t + D], m.ident[0:NP, 0:NP])
                tr.then_inc(y_turned, 1)

            def first_y(q, s, turn):
                turn_x(q, s)
                times_w(q, s)

            def step_y(q, s, turn):
                turn_x(q + 1, 1 - s)
                times_w(q + 1, 1 - s)
                turn_y(q, s)
            pipelined(pe, NB, first_y, step_y, lambda q, s, turn: turn_y(q, s))

        @block.gpsimd
        def _(pool):
            pool.sem_inc(x_kept, 2)

            def keep(q, s, turn):
                pool.wait_ge(x_done, ready(q, 0))
                pool.sem_inc(x_seen, 1)
                nc.gpsimd.tensor_copy(m.xs_flat[:, bass.ds(q * (B * D), B * D)], xn[s]).then_inc(x_kept, 1)
            over(pool, NB, keep)

        @block.scalar
        def _(act):
            act.wait_ge(dinv_steps, 1)
            nc.scalar.activation(m.dinv[:, :], m.dinv[:, :], ACT.Sqrt).then_inc(dinv_act, 1)
            act.preload_act_table_set("natural_log_exp_and_others")
            act.sem_inc(agg_copied, 2)
            act.sem_inc(ln_made, 2)

            def step(q, s, turn):
                act.wait_ge(agg_turned, ready(q, 2))
                act.wait_ge(hid_made, free(q))
                nc.scalar.copy(aggT[s], ps_a[s]).then_inc(agg_copied, 1)
                act.wait_ge(hid_made, ready(q, 2))
                act.wait_ge(hid_done, free(q))
                nc.scalar.activation(log1p, ps_h[s], ACT.Abs, bias=m.bo1_s[:, 0:1]).then_inc(act_steps, 1)
                nc.scalar.activation(relu, ps_h[s], ACT.Relu, bias=m.bo1_s[:, 0:1])
                act.wait_ge(act_steps, 2 * q + 1)
                nc.scalar.activation(log1p, log1p, ACT.Exp, scale=-1.0).then_inc(act_steps, 1)
                act.wait_ge(act_steps, 2 * q + 2)
                nc.scalar.activation(log1p, log1p, ACT.Ln, scale=0.5, bias=m.half[:, 0:1]).then_inc(ln_made, 1)
            over(act, NB, step)

            act.wait_ge(var_done, 1)
            nc.scalar.activation(rstd, var, ACT.Sqrt).then_inc(std_done, 1)
            act.sem_inc(xT_copied, 2)
            act.sem_inc(y_scaled, 1)
            act.sem_inc(y_stored[0], 16)
            act.sem_inc(y_stored[1], 16)
            act.wait_ge(dinv_steps, 2)

            def step_y(q, s, turn):
                act.wait_ge(x_turned, ready(q, 2))
                act.wait_ge(y_made, free(q))
                nc.scalar.copy(xT[s], ps_xT[s]).then_inc(xT_copied, 1)
                act.wait_ge(y_made, ready(q, 2))
                act.wait_ge(y_stored[s], 16 * turn + 16)
                act.wait_ge(y_turned, free(q))
                for t in range(B):
                    last = nc.scalar.activation(yb[s][:, D * t:D * t + D], ps_y[s][:, D * t:D * t + D], ACT.Copy,
                                                scale=m.dinv[:, bass.ds(q * B + t, 1)])
                last.then_inc(y_scaled, 1)
            over(act, NB, step_y)

        @block.vector
        def _(dve):
            dve.sem_inc(agg_sum, 2)
            dve.sem_inc(hid_done, 1)
            dve.sem_inc(res_done, 2)
            dve.wait_ge(deg_in, 32)
            nc.vector.scalar_tensor_tensor(m.dinv[:, :], m.dinv[:, :], 1.0, deg2, ALU.add, ALU.add).then_inc(dinv_steps, 1)
            nc.vector.memset(m.arena[:, N:NT], 0.0)
            dve.wait_ge(dinv_act, 1)
            nc.vector.reciprocal(m.dinv[:, :], m.dinv[:, :]).then_inc(dinv_steps, 1)

            def sum_tables(q, s, turn):
                dve.wait_ge(tabs_in[s], 16 * K * (turn + 1))
                dve.wait_ge(agg_turned, free(q))
                nc.vector.tensor_reduce(agg[s], tabs[s].rearrange("p (k n) -> p n k", k=K), AX.X,
                                        ALU.add).then_inc(agg_sum, 1)

            def add_hidden(q, s, turn):
                dve.wait_ge(ln_made, ready(q, 2))
                dve.wait_ge(out_made, free(q))
                nc.vector.tensor_tensor(hid[s], relu, log1p, ALU.add).then_inc(hid_done, 1)

            def residual(q, s, turn):
                dve.wait_ge(out_made, ready(q, 2))
                here = m.xs_flat[:, bass.ds(q * (B * D), B * D)]
                nc.vector.tensor_tensor(here, here, ps_o[s], ALU.add).then_inc(res_done, 1)
                dve.wait_ge(res_done, ready(q, 2))
                layer_norm_stats(nc, dve, m, LN_AT, steps, waited, 3 * q, q, s, mv)

            def first(q, s, turn):
                sum_tables(q, s, turn)
                add_hidden(q, s, turn)

            def step(q, s, turn):
                sum_tables(q + 1, 1 - s, turn + s)
                add_hidden(q + 1, 1 - s, turn + s)
                residual(q, s, turn)
            pipelined(dve, NB, first, step, residual)
            dve.wait_ge(steps, 3 * NB)
            mvv = mv.rearrange("p (c s) -> p c s", s=2)
            nc.vector.tensor_scalar(var, mvv[:, :, 1], LN_EPS, None, ALU.add).then_inc(var_done, 1)
            dve.wait_ge(std_done, 1)
            nc.vector.reciprocal(rstd, rstd).then_inc(rstd_done, 1)
            dve.wait_ge(rstd_done, 1)
            dve.sem_inc(yT_copied, 2)

            def norm(q, s, turn):
                dve.wait_ge(x_kept, free(q))
                dve.wait_ge(x_turned, free(q))
                for t in range(B):
                    here = m.xs_flat[:, bass.ds(q * (B * D) + t * D, D)]
                    last = nc.vector.tensor_scalar(xn[s][:, D * t:D * t + D], here, mv[:, bass.ds(q * (2 * B) + 2 * t, 1)],
                                                   rstd[:, bass.ds(q * B + t, 1)], ALU.subtract, ALU.mult)
                last.then_inc(x_done, 1)

            def keep_yT(q, s, turn):
                dve.wait_ge(y_turned, ready(q, 2))
                nc.vector.tensor_copy(rows[:, bass.ds(q * B, B), :], ps_yT[s].rearrange("f (t p) -> f t p", t=B)).then_inc(yT_copied, 1)

            def step_y(q, s, turn):
                norm(q + 1, 1 - s, turn)
                keep_yT(q, s, turn)
            pipelined(dve, NB, norm, step_y, keep_yT)


def graph_layer(nc, m, io):
    ps, work = m.ps, m.work

    def slots(at, width):
        return [work[:, at + width * s:at + width * s + width] for s in range(2)]

    grow = slots(0, J * D)
    pick = slots(2048, J * P)
    gidx = [v.bitcast(U32) for v in slots(4096, J)]
    place = slots(4112, J)
    drow = [v[0:2, :].bitcast(BF16) for v in slots(4160, GE // 2)]
    same = slots(2048, J * P)
    summed = slots(5200, J * D)
    sidx = [v.bitcast(U32) for v in slots(7250, J)]
    earlier = slots(7270, J)
    first = work[:, 7290:7290 + J]
    dstT = work[:, 7300:7300 + J]
    tabs = work[0:NP, 7400:7400 + K * B * D]
    total = work[0:NP, 9448:9448 + B * D]
    ps_win = [ps[:, s, 0:P] for s in range(2)]
    ps_sum = ps[:, 2:4, :].rearrange("p a b -> p (a b)")
    ps_dst = ps[:, 4:6, :].rearrange("p a b -> p (a b)")
    ps_tot = ps[:, 6, 0:BW]
    rows = m.arena[:, 0:N].rearrange("f (p c) -> f c p", c=NC)

    with ExitStack() as ctx:
        def sem(name):
            return ctx.enter_context(nc.semaphore(name))
        gathered = [sem("y_gathered0"), sem("y_gathered1")]
        loaded = [sem("dst_loaded0"), sem("dst_loaded1")]
        gidx_done, place_done, pick_done = sem("y_idx_done"), sem("place_done"), sem("y_pick_done")
        win_made, win_added, pool_turn = sem("window_made"), sem("window_added"), sem("y_pool_turn")
        dst_out, same_done, first_done, idx_done = sem("dst_out"), sem("y_same"), sem("y_first"), sem("y_sidx")
        sum_made, sum_copied, dstT_done = sem("y_sum_made"), sem("y_sum_copied"), sem("dstT_done")
        tabs_in, tot_done, tot_turned, tot_added = sem("y_tabs_in"), sem("tot_done"), sem("tot_turned"), sem("tot_added")
        all_added = sem("all_scattered")
        block = ctx.enter_context(nc.Block())

        def gather(pool, g, s, turn, used):
            pool.wait_ge(gidx_done, ready(g, 0))
            pool.wait_ge(used, free(g))
            pool.sem_inc(pool_turn, 1)
            for j in range(J):
                nc.gpsimd.indirect_dma_start(
                    out=grow[s][:, D * j:D * j + D], out_offset=None, in_=m.y_tab[:, :],
                    in_offset=bass.IndirectOffsetOnAxis(ap=gidx[s][:, j:j + 1], axis=0)).then_inc(gathered[s], 16)

        def scatter(pool, g, s, turn):
            pool.wait_ge(idx_done, ready(g, 0))
            pool.wait_ge(sum_copied, ready(g, 1))
            for j in range(J):
                k = j % K
                pool.wait_ge(m.out_added[k], 32 * g + 16 * (j // K) + ZEROED)
                pool.sem_inc(pool_turn, 1)
                nc.gpsimd.indirect_dma_start(
                    out=m.out_tab[k][:, :], out_offset=bass.IndirectOffsetOnAxis(ap=sidx[s][:, j:j + 1], axis=0),
                    in_=summed[s][:, D * j:D * j + D], in_offset=None,
                    compute_op=ALU.add).then_inc(m.out_added[k], 16)

        @block.gpsimd
        def _(pool):
            flag = pool.value_load(m.flag_i[0:1, 0:1], min_val=0, max_val=1)
            with pool.If(flag == 1):
                over(pool, G, lambda g, s, turn: gather(pool, g, s, turn, win_made))
            with pool.Else():
                for k in range(K):
                    zero_table(pool, m.out_tab[k], D, m.zeros, m.out_added[k])

                def step(g, s, turn):
                    gather(pool, g + 1, 1 - s, turn + s, sum_made)
                    scatter(pool, g, s, turn)
                pipelined(pool, G, lambda g, s, turn: gather(pool, g, s, turn, sum_made), step,
                          lambda g, s, turn: scatter(pool, g, s, turn))
                for k in range(K):
                    pool.wait_ge(m.out_added[k], 32 * G + ZEROED)
                pool.sem_inc(all_added, 1)
            pool.wait_ge(pool_turn, G)

        @block.tensor
        def _(pe):
            pe.sem_inc(win_made, 2)
            pe.sem_inc(sum_made, 2)
            flag = pe.value_load(m.flag_i[0:1, 0:1], min_val=0, max_val=1)
            with pe.If(flag == 1):
                def window(g, s, turn):
                    pe.wait_ge(gathered[s], 128 * turn + 128)
                    pe.wait_ge(pick_done, ready(g, 0))
                    pe.wait_ge(win_added, free(g))
                    for j in range(J):
                        mm = pe.matmul(ps_win[s], grow[s][:, D * j:D * j + D], pick[s][:, P * j:P * j + P],
                                       start=(j == 0), stop=(j == J - 1))
                    mm.then_inc(win_made, 1)
                over(pe, G, window)
            with pe.Else():
                def spread(g, s, turn):
                    pe.wait_ge(loaded[s], 16 * turn + 16)
                    pe.wait_ge(same_done, free(g))
                    for q in range(2):
                        mm = pe.matmul(ps_dst[:, 512 * q:512 * q + 512], m.split[:, :], drow[s][:, 512 * q:512 * q + 512],
                                       start=True, stop=True)
                    mm.then_inc(dst_out, 1)

                def sums(g, s, turn):
                    pe.wait_ge(same_done, ready(g, 1))
                    pe.wait_ge(gathered[s], 128 * turn + 128)
                    pe.wait_ge(sum_copied, free(g))
                    for j in range(J):
                        mm = pe.matmul(ps_sum[:, D * j:D * j + D], same[s][:, P * j:P * j + P], grow[s][:, D * j:D * j + D],
                                       start=True, stop=True)
                    mm.then_inc(sum_made, 1)

                def step(g, s, turn):
                    spread(g + 1, 1 - s, turn + s)
                    sums(g, s, turn)
                pipelined(pe, G, spread, step, sums)
                with pe.Fori(0, NB) as q:
                    pe.wait_ge(tot_done, q + 1)
                    for t in range(B):
                        tr = pe.transpose(ps_tot[:, NP * t:NP * t + NP], total[:, D * t:D * t + D], m.ident[0:NP, 0:NP])
                    tr.then_inc(tot_turned, 1)
            pe.wait_ge(gathered[0], 128)

        @block.sync
        def _(sp):
            flag = sp.value_load(m.flag_i[0:1, 0:1], min_val=0, max_val=1)
            with sp.If(flag == 0):
                def load(g, s, turn):
                    sp.wait_ge(same_done, g)
                    sp.dma_start(drow[s], m.dst_hl[bass.ds(g, 1), :, :].rearrange("o t e -> (o t) e")).then_inc(loaded[s], 16)
                sp.dma_start(drow[0], m.dst_hl[0, :, :]).then_inc(loaded[0], 16)
                sp.dma_start(drow[1], m.dst_hl[1, :, :]).then_inc(loaded[1], 16)
                with sp.Fori(0, (G - 3) // 2) as i:
                    load(2 * i + 2, 0, None)
                    load(2 * i + 3, 1, None)
                load(G - 1, 0, None)
                sp.wait_ge(all_added, 1)
                with sp.Fori(0, NB) as q:
                    sp.wait_ge(tot_added, q + 1)
                    for k in range(K):
                        sp.dma_start(tabs[:, B * D * k:B * D * k + B * D],
                                     m.out_tab[k][0:N, :].rearrange("(p c) d -> p (c d)", p=NP)[:, bass.ds(q * (B * D), B * D)]
                                     ).then_inc(tabs_in, 16)
            with sp.Else():
                sp.sem_inc(all_added, 1)
            sp.wait_ge(all_added, 1)

        @block.scalar
        def _(act):
            flag = act.value_load(m.flag_i[0:1, 0:1], min_val=0, max_val=1)
            with act.If(flag == 0):
                act.sem_inc(sum_copied, 1)
                for k in range(K):
                    act.wait_ge(m.out_added[k], ZEROED)

                def copy(g, s, turn):
                    act.wait_ge(sum_made, ready(g, 2))
                    for k in range(K):
                        act.wait_ge(m.out_added[k], 32 * g + ZEROED - 32)
                    nc.scalar.copy(summed[s], ps_sum).then_inc(sum_copied, 1)
                over(act, G, copy)
            with act.Else():
                act.sem_inc(all_added, 1)
            act.wait_ge(all_added, 1)

        def same_rows(dve, g, s):
            dve.wait_ge(dst_out, ready(g, 0))
            dve.wait_ge(sum_made, free(g))
            for j in range(J):
                mm = nc.vector.scalar_tensor_tensor(same[s][:, P * j:P * j + P], ps_dst.rearrange("p (e j) -> p j e", j=J)[:, j, :],
                                                    m.dstF[:, bass.ds(g * J + j, 1)], m.below[:, :], ALU.is_equal, ALU.mult,
                                                    accum_out=earlier[s][:, j:j + 1])
            mm.then_inc(same_done, 1)
            nc.vector.tensor_scalar(dstT, m.dstF[:, bass.ds(g * J, J)], m.trash[:, 0:1], None, ALU.subtract).then_inc(dstT_done, 1)
            dve.wait_ge(same_done, ready(g, 1))
            dve.wait_ge(dstT_done, ready(g, 0))
            nc.vector.scalar_tensor_tensor(first, earlier[s], 1.0, dstT, ALU.is_equal, ALU.mult).then_inc(first_done, 1)
            dve.wait_ge(first_done, ready(g, 0))
            for k in range(K):
                dve.wait_ge(m.out_added[k], 32 * g + ZEROED - 32)
            nc.vector.tensor_scalar(sidx[s], first, m.trash[:, 0:1], None, ALU.add).then_inc(idx_done, 1)

        def indices(dve, g, s, turn, used):
            dve.wait_ge(used, free(g))
            nc.vector.tensor_copy(gidx[s], m.srcF[:, bass.ds(g * J, J)]).then_inc(gidx_done, 1)

        @block.vector
        def _(dve):
            dve.sem_inc(win_added, 2)
            dve.sem_inc(same_done, 1)
            flag = dve.value_load(m.flag_i[0:1, 0:1], min_val=0, max_val=1)
            with dve.If(flag == 1):
                def front(g, s, turn):
                    indices(dve, g, s, turn, win_made)
                    nc.vector.tensor_scalar(place[s], m.dstF[:, bass.ds(g * J, J)], m.base_bc[:, bass.ds(g, 1)], None,
                                            ALU.subtract).then_inc(place_done, 1)
                    dve.wait_ge(place_done, ready(g, 0))
                    dve.wait_ge(win_made, free(g))
                    nc.vector.tensor_tensor(pick[s].rearrange("p (j w) -> p j w", j=J),
                                            m.iota_w[:, :].unsqueeze(1).to_broadcast([P, J, P]),
                                            place[s].unsqueeze(2).to_broadcast([P, J, P]), ALU.is_equal).then_inc(pick_done, 1)

                def back(g, s, turn):
                    base = dve.value_load(m.base_i[0:1, bass.ds(g, 1)], min_val=0, max_val=N)
                    dve.wait_ge(win_made, ready(g, 2))
                    here = m.arena[:, bass.ds(base, P)]
                    nc.vector.tensor_tensor(here, here, ps_win[s], ALU.add).then_inc(win_added, 1)
                    dve.wait_ge(win_added, ready(g, 2))

                def step(g, s, turn):
                    front(g + 1, 1 - s, turn + s)
                    back(g, s, turn)
                pipelined(dve, G, front, step, back)
            with dve.Else():
                def gfront(g, s, turn):
                    indices(dve, g, s, turn, sum_made)
                    same_rows(dve, g, s)
                for k in range(K):
                    dve.wait_ge(m.out_added[k], ZEROED)
                over(dve, G, gfront)
                dve.sem_inc(tot_added, 1)
                with dve.Fori(0, NB) as q:
                    dve.wait_ge(tabs_in, q * (16 * K) + 16 * K)
                    nc.vector.tensor_reduce(total, tabs.rearrange("p (k n) -> p n k", k=K), AX.X, ALU.add).then_inc(tot_done, 1)
                    dve.wait_ge(tot_turned, q + 1)
                    here = rows[:, bass.ds(q * B, B), :]
                    nc.vector.tensor_tensor(here, here, ps_tot.rearrange("f (t p) -> f t p", t=B), ALU.add).then_inc(tot_added, 1)
            dve.wait_ge(gidx_done, G)


def norm_and_store(nc, m, io):
    ps, work = m.ps, m.work
    drow = [work[0:1, 512 * s:512 * s + BW] for s in range(2)]
    stats = work[:, 1024:1024 + 6 * NB]
    mean_var = work[:, 1200:1202]
    std, scale, shift = work[:, 1202:1203], work[:, 1203:1204], work[:, 1204:1205]
    var_eps, mean_scale = work[:, 1205:1206], work[:, 1206:1207]
    turned = [work[:, 1536 + 512 * s:1536 + 512 * s + BW] for s in range(2)]
    LN_AT = 2600
    mv = work[0:NP, 2700:2700 + 2 * NC]
    rstd = work[0:NP, 2900:2900 + NC]
    var = work[0:NP, 3000:3000 + NC]
    ps_d = [ps[:, s, 0:BW] for s in range(2)]
    ps_r = [ps[0:NP, 2 + s, :] for s in range(2)]
    rows = m.arena[:, 0:N].rearrange("f (p c) -> f c p", c=NC)
    with ExitStack() as ctx:
        def sem(name):
            return ctx.enter_context(nc.semaphore(name))
        row_in = [sem("dinv_row0"), sem("dinv_row1")]
        spread, scaled, bn_steps, bn_agg = sem("dinv_spread"), sem("sums_scaled"), sem("bn_steps"), sem("bn_aggregated")
        bn_std, bn_ready = sem("bn_std"), sem("bn_ready")
        relu_done, turned_back, res_done, steps = sem("relu_done"), sem("turned_back"), sem("residual2"), sem("ln2_steps")
        waited = sem("ln2_waited")
        var_done, std_done, rstd_done, x_done, stored = (
            sem("var2_done"), sem("std2_done"), sem("rstd2_done"), sem("x2_done"), sem("out_stored"))
        block = ctx.enter_context(nc.Block())

        @block.sync
        def _(sp):
            def load(q, s, turn):
                sp.wait_ge(spread, free(q))
                sp.dma_start(drow[s], m.dinv_tab[bass.ds(q * BW, BW)].rearrange("(o n) -> o n", o=1)).then_inc(row_in[s], 16)
            over(sp, NB, load)
            flat = io["out"].rearrange("(p c) d -> p (c d)", p=NP)
            with sp.Fori(0, NB) as q:
                sp.wait_ge(x_done, q + 1)
                sp.dma_start(flat[:, bass.ds(q * (B * D), B * D)], m.xs_flat[:, bass.ds(q * (B * D), B * D)]).then_inc(stored, 16)
            sp.wait_ge(stored, 16 * NB)

        @block.tensor
        def _(pe):
            pe.sem_inc(spread, 2)

            def row(q, s, turn):
                pe.wait_ge(row_in[s], 16 * turn + 16)
                pe.wait_ge(scaled, free(q))
                pe.matmul(ps_d[s], m.ones[:, :], drow[s], start=True, stop=True).then_inc(spread, 1)
            over(pe, NB, row)
            pe.sem_inc(turned_back, 2)

            def back(q, s, turn):
                pe.wait_ge(relu_done, ready(q, 0))
                pe.wait_ge(res_done, free(q))
                for t in range(B):
                    tr = pe.transpose(ps_r[s][:, D * t:D * t + D], turned[s][:, NP * t:NP * t + NP], m.ident[:, :])
                tr.then_inc(turned_back, 1)
            over(pe, NB, back)

        @block.scalar
        def _(act):
            act.wait_ge(bn_agg, 2)
            nc.scalar.activation(std, var_eps, ACT.Sqrt).then_inc(bn_std, 1)
            act.wait_ge(bn_ready, 4)

            def normed(q, s, turn):
                act.wait_ge(turned_back, free(q))
                nc.scalar.activation(turned[s].rearrange("f (t p) -> f t p", t=B), rows[:, bass.ds(q * B, B), :], ACT.Relu,
                                     bias=shift, scale=scale).then_inc(relu_done, 1)
            over(act, NB, normed)
            act.wait_ge(var_done, 1)
            nc.scalar.activation(rstd, var, ACT.Sqrt).then_inc(std_done, 1)

        @block.vector
        def _(dve):
            dve.sem_inc(scaled, 2)

            def scale_sums(q, s, turn):
                here = m.arena[:, bass.ds(q * BW, BW)]
                dve.wait_ge(spread, ready(q, 2))
                nc.vector.tensor_tensor(here, here, ps_d[s], ALU.mult).then_inc(scaled, 1)
                dve.wait_ge(scaled, ready(q, 2))
                nc.vector.tensor_scalar(here, here, m.gbb[:, 0:1], None, ALU.add).then_inc(bn_steps, 1)
                dve.wait_ge(bn_steps, 2 * q + 1)
                dve.sem_inc(waited, 1)
                nc.vector.bn_stats(stats[:, bass.ds(q * 6, 6)], here).then_inc(bn_steps, 1)
            over(dve, NB, scale_sums)
            dve.wait_ge(bn_steps, 2 * NB)
            nc.vector.bn_aggr(mean_var, stats).then_inc(bn_agg, 1)
            dve.wait_ge(bn_agg, 1)
            nc.vector.tensor_scalar(var_eps, mean_var[:, 1:2], BN_EPS, None, ALU.add).then_inc(bn_agg, 1)
            dve.wait_ge(bn_std, 1)
            nc.vector.reciprocal(std, std).then_inc(bn_ready, 1)
            dve.wait_ge(bn_ready, 1)
            nc.vector.tensor_tensor(scale, std, m.gbb[:, 1:2], ALU.mult).then_inc(bn_ready, 1)
            dve.wait_ge(bn_ready, 2)
            nc.vector.tensor_tensor(mean_scale, mean_var[:, 0:1], scale, ALU.mult).then_inc(bn_ready, 1)
            dve.wait_ge(bn_ready, 3)
            nc.vector.tensor_tensor(shift, m.gbb[:, 2:3], mean_scale, ALU.subtract).then_inc(bn_ready, 1)
            dve.sem_inc(res_done, 2)

            def residual(q, s, turn):
                dve.wait_ge(turned_back, ready(q, 2))
                here = m.xs_flat[:, bass.ds(q * (B * D), B * D)]
                nc.vector.tensor_tensor(here, here, ps_r[s], ALU.add).then_inc(res_done, 1)
                dve.wait_ge(res_done, ready(q, 2))
                layer_norm_stats(nc, dve, m, LN_AT, steps, waited, 3 * q, q, s, mv)
            over(dve, NB, residual)
            dve.wait_ge(steps, 3 * NB)
            nc.vector.tensor_scalar(var, mv.rearrange("p (c s) -> p c s", s=2)[:, :, 1], LN_EPS, None, ALU.add).then_inc(var_done, 1)
            dve.wait_ge(std_done, 1)
            nc.vector.reciprocal(rstd, rstd).then_inc(rstd_done, 1)
            dve.wait_ge(rstd_done, 1)
            with dve.Fori(0, NB) as q:
                for t in range(B):
                    here = m.xs_flat[:, bass.ds(q * (B * D) + t * D, D)]
                    last = nc.vector.tensor_scalar(here, here, mv[:, bass.ds(q * (2 * B) + 2 * t, 1)],
                                                   rstd[:, bass.ds(q * B + t, 1)], ALU.subtract, ALU.mult)
                last.then_inc(x_done, 1)


def program(nc, io):
    with ExitStack() as ctx:
        m = Memory(nc, ctx)
        setup(nc, m, io)
        filter_layer(nc, m, io)
        node_update(nc, m, io)
        graph_layer(nc, m, io)
        norm_and_store(nc, m, io)


def kernel(**inputs):
    import numpy as np
    import concourse.bacc as bacc
    from concourse.bass_utils import run_bass_kernel_spmd

    nc = bacc.Bacc("TRN2", target_bir_lowering=False, num_devices=1)
    arrays, io = {}, {}
    for name, given in INPUTS.items():
        a = np.ascontiguousarray(inputs[given])
        arrays[f"in_{name}"] = a
        io[name] = nc.dram_tensor(f"in_{name}", a.shape, mybir.dt.from_np(a.dtype), kind="ExternalInput").ap()
    io["out"] = nc.dram_tensor("out", (N, D), F32, kind="ExternalOutput").ap()
    program(nc, io)
    r = run_bass_kernel_spmd(nc, [arrays], core_ids=[0])
    return r.results[0]["out"]
```
